# Optimizing a Trainium2 kernel written in Bass

```python
import numpy as np
import jax
import jax.numpy as jnp

def _softmax(x, axis=-1):
    return jax.nn.softmax(x, axis=axis)

def _gelu(x):
    return jax.nn.gelu(x, approximate=True)

def _silu(x):
    return jax.nn.silu(x)

def _sigmoid(x):
    return jax.nn.sigmoid(x)

def _layernorm(x, axis=-1, eps=1e-05):
    m = jnp.mean(x, axis=axis, keepdims=True)
    v = jnp.var(x, axis=axis, keepdims=True)
    return (x - m) / jnp.sqrt(v + eps)

def _scatter_add(tgt, idx, src, axis=0):
    return tgt.at[idx].add(src)

def _segment_sum(src, seg, n):
    return jax.ops.segment_sum(src, seg, n)
kernel_name = 'mk_adaln_d1_jaxref_r8_dbde34'

def setup_inputs(seed: int=0):
    np.random.seed(seed)
    _w = jnp.asarray

    def _L0_attn_setup():
        import jax, jax.numpy as jnp
        import numpy as np
        D_MODEL = 128
        NUM_HEADS = 16
        D_K = D_MODEL // NUM_HEADS
        ROPE_THETA = 10000.0

        def _apply_rope(t):
            S, dk = (t.shape[-2], t.shape[-1])
            inv_freq = 1.0 / ROPE_THETA ** (jnp.arange(0, dk, 2) / dk)
            angles = jnp.outer(jnp.arange(S), inv_freq)
            cos = jnp.repeat(jnp.cos(angles), 2, axis=-1).astype(t.dtype)
            sin = jnp.repeat(jnp.sin(angles), 2, axis=-1).astype(t.dtype)
            t_even = t[..., 0::2]
            t_odd = t[..., 1::2]
            t_rot = jnp.stack([-t_odd, t_even], axis=-1).reshape(t.shape)
            return t * cos + t_rot * sin
        key = jax.random.key(seed)
        kx, kq, kk, kv, ko = jax.random.split(key, 5)
        B, S = (4, 256)
        std = (2.0 / (D_MODEL + D_MODEL)) ** 0.5

        def w(k):
            return jax.random.truncated_normal(k, -3.0, 3.0, (D_MODEL, D_MODEL), jnp.float32) * std
        return {'x': jax.random.normal(kx, (B, S, D_MODEL), jnp.float32), 'Wq': w(kq), 'Wk': w(kk), 'Wv': w(kv), 'Wo': w(ko)}
    _L0_attn_in = _L0_attn_setup()

    def _L0_ffn_setup():
        import jax, jax.numpy as jnp
        import numpy as np
        B, S, D, T = (4, 512, 128, 8)
        key = jax.random.key(seed)
        k1, k2, k3, k4 = jax.random.split(key, 4)
        x = jax.random.normal(k1, (B, S, D), dtype=jnp.float32)
        tile_sigs = jax.random.normal(k2, (T, D), dtype=jnp.float32)
        bound = 1.0 / np.sqrt(D)
        W = jax.random.uniform(k3, (T, D, D), minval=-bound, maxval=bound, dtype=jnp.float32)
        b = jax.random.uniform(k4, (T, D), minval=-bound, maxval=bound, dtype=jnp.float32)
        return {'x': x, 'tile_sigs': tile_sigs, 'W': W, 'b': b}
    _L0_ffn_in = _L0_ffn_setup()
    _L0_c = _w((lambda *s: np.random.randn(*s).astype(np.float32) * 0.05)(2, 128))
    _L0_wmod = _w((lambda *s: np.random.randn(*s).astype(np.float32) * 0.05)(128, 6 * 128) * 128 ** (-0.5))
    _d = {'L0_attn_x': _L0_attn_in['x'], 'L0_attn_Wq': _L0_attn_in['Wq'], 'L0_attn_Wk': _L0_attn_in['Wk'], 'L0_attn_Wv': _L0_attn_in['Wv'], 'L0_attn_Wo': _L0_attn_in['Wo'], 'L0_ffn_tile_sigs': _L0_ffn_in['tile_sigs'], 'L0_ffn_W': _L0_ffn_in['W'], 'L0_ffn_b': _L0_ffn_in['b'], 'L0_c': _L0_c, 'L0_wmod': _L0_wmod}
    _x0 = _d['L0_attn_x']
    _d['L0_attn_x'] = jax.random.normal(jax.random.fold_in(jax.random.key(seed), 1), (2, 1024, 128), dtype=_x0.dtype)
    del _x0
    return _d

def reference(L0_attn_x, L0_attn_Wq, L0_attn_Wk, L0_attn_Wv, L0_attn_Wo, L0_ffn_tile_sigs, L0_ffn_W, L0_ffn_b, L0_c, L0_wmod):

    def _L0_attn_ref(x, Wq, Wk, Wv, Wo):
        import jax, jax.numpy as jnp
        import numpy as np
        D_MODEL = 128
        NUM_HEADS = 16
        D_K = D_MODEL // NUM_HEADS
        ROPE_THETA = 10000.0

        def _apply_rope(t):
            S, dk = (t.shape[-2], t.shape[-1])
            inv_freq = 1.0 / ROPE_THETA ** (jnp.arange(0, dk, 2) / dk)
            angles = jnp.outer(jnp.arange(S), inv_freq)
            cos = jnp.repeat(jnp.cos(angles), 2, axis=-1).astype(t.dtype)
            sin = jnp.repeat(jnp.sin(angles), 2, axis=-1).astype(t.dtype)
            t_even = t[..., 0::2]
            t_odd = t[..., 1::2]
            t_rot = jnp.stack([-t_odd, t_even], axis=-1).reshape(t.shape)
            return t * cos + t_rot * sin
        B, S, D = x.shape
        H, dk = (NUM_HEADS, D_K)
        q = jnp.einsum('bsi,io->bso', x, Wq).reshape(B, S, H, dk).swapaxes(1, 2)
        k = jnp.einsum('bsi,io->bso', x, Wk).reshape(B, S, H, dk).swapaxes(1, 2)
        v = jnp.einsum('bsi,io->bso', x, Wv).reshape(B, S, H, dk).swapaxes(1, 2)
        q = _apply_rope(q)
        k = _apply_rope(k)
        scores = jnp.einsum('bhqd,bhkd->bhqk', q, k) / dk ** 0.5
        causal = jnp.tril(jnp.ones((S, S), dtype=bool))
        scores = jnp.where(causal, scores, -jnp.inf)
        attn = jax.nn.softmax(scores, axis=-1)
        out = jnp.einsum('bhqk,bhkd->bhqd', attn, v)
        out = out.swapaxes(1, 2).reshape(B, S, D)
        return jnp.einsum('bsi,io->bso', out, Wo)

    def _L0_ffn_ref(x, tile_sigs, W, b):
        import jax, jax.numpy as jnp
        import numpy as np
        B, S, D, T = (4, 512, 128, 8)
        scores = jnp.einsum('bsd,td->bst', x, jnp.sign(tile_sigs))
        idx = jnp.argmax(scores, axis=-1)
        all_out = jnp.einsum('bsd,tde->bste', x, W) + b[None, None]
        out = jnp.take_along_axis(all_out, idx[:, :, None, None], axis=2)
        return out[:, :, 0, :]
    x = L0_attn_x
    mod = (_silu(L0_c) @ L0_wmod).reshape(L0_c.shape[0], 6, 1, -1)
    sa, ca, ga, sb, cb, gb = (mod[:, 0], mod[:, 1], mod[:, 2], mod[:, 3], mod[:, 4], mod[:, 5])
    ga = (2 * (ga >= 0) - 1) * jnp.maximum(jnp.abs(ga), 0.25)
    gb = (2 * (gb >= 0) - 1) * jnp.maximum(jnp.abs(gb), 0.25)
    h = _layernorm(x, axis=-1) * (1 + ca) + sa
    x = x + ga * _L0_attn_ref(h, L0_attn_Wq, L0_attn_Wk, L0_attn_Wv, L0_attn_Wo)
    h = _layernorm(x, axis=-1) * (1 + cb) + sb
    x = x + gb * _L0_ffn_ref(h, L0_ffn_tile_sigs, L0_ffn_W, L0_ffn_b)
    return x

_drawn_inputs = setup_inputs


def setup_inputs(seed=0):
    import zlib

    import numpy as np

    out = dict(_drawn_inputs(seed))
    spreads = {}
    factors = {'L0_ffn_b': 4.694}
    for name, (base, spread) in spreads.items():
        noise = np.random.default_rng([zlib.crc32(name.encode()), seed]).standard_normal(out[name].shape)
        drawn = base * np.exp(spread * noise) if base else spread * noise
        out[name] = jnp.asarray(drawn.astype(out[name].dtype))
    for name, factor in factors.items():
        out[name] = (out[name] * factor).astype(out[name].dtype)
    return out
```

```python
from contextlib import ExitStack

import numpy as np

import concourse.bass as bass
from concourse import mybir

F32 = mybir.dt.float32
BF16 = mybir.dt.bfloat16
ALU = mybir.AluOpType
ACT = mybir.ActivationFunctionType
AX_X = mybir.AxisListType.X

P = 128
BATCH, SEQ, D = 2, 1024, 128
HEADS = 16
DK = D // HEADS
EXPERTS = 8
TILES = SEQ // P
CHUNK = 512
CT = CHUNK // P
GH = 4
GROUPS = BATCH * HEADS // GH
GPB = HEADS // GH
SCALE = float(DK) ** -0.5
EPS = 1e-5
COMBOS = 6
Q_PART = [0, 0, 0, 1, 1, 2]
K_PART = [0, 1, 2, 0, 1, 0]
SROWS = COMBOS * DK
ZROWS = 96
MROW = ZROWS
VW = 32
NEG = -1.0e30



def max_items():
    hi = [("diag", h, (i,)) for i in (4, 6) for h in (0, 1)]
    hi += [("wide", h, (6, 4)) for h in (0, 1)] + [("wide", h, (7, 5)) for h in (0, 1)]
    hi += [("two", h, (5, 4, 7, 4)) for h in (0, 1)]
    hi += [("full", h, (i, pr)) for i in range(4, 8) for pr in (0, 1) for h in (0, 1)]
    lo = [("diag", h, (i,)) for i in (0, 2) for h in (0, 1)]
    lo += [("wide", h, (2, 0)) for h in (0, 1)] + [("wide", h, (3, 1)) for h in (0, 1)]
    lo += [("two", h, (1, 0, 3, 0)) for h in (0, 1)]
    return hi, lo


HI, LO = max_items()
ITEMS = HI + LO
NI, NHI = len(ITEMS), len(HI)

STEPS = [(1, j) for j in range(8)] + [(0, j) for j in range(4)]
NS = len(STEPS)
PRING = 3
SHARE = [5, 5, 4, 4, 4, 2, 1, 1, 4, 3, 2, 1]
assert sum(SHARE) == NI and NS % PRING == 0


def held_by(engine, always, count, *waits):
    counts = [(s, n if isinstance(n, int) else engine.to_reg(n)) for s, n in waits]
    engine.wait_ge(always, count)
    for s, n in counts:
        engine.wait_ge(s, n)


def rope_tables():
    inv = (1.0 / np.float32(10000.0) ** (np.arange(0, DK, 2, dtype=np.float32) / np.float32(DK))).astype(np.float32)
    ang = np.outer(np.arange(SEQ, dtype=np.float32), inv).astype(np.float32)
    cos = np.repeat(np.cos(ang), 2, axis=-1)
    sin = np.repeat(np.sin(ang), 2, axis=-1)
    sin[:, 0::2] *= -1.0
    both = np.stack([cos, sin]).astype(np.float32).reshape(2, TILES, P, DK)
    return np.ascontiguousarray(both.transpose(2, 0, 1, 3))


def adaln_block_kernel(nc, x, wq, wk, wv, wo, sigs, w_ffn, b_ffn, cond, wmod, rope, out):
    x_t = x.rearrange("b (t p) d -> p (b t) d", p=P)
    out_t = out.rearrange("b (t p) d -> p (b t) d", p=P)
    parts_dram = nc.dram_tensor("parts_dram", (2, GROUPS * GH, COMBOS, DK, SEQ), BF16).ap()

    with ExitStack() as ctx:
        def sb(name, shape, dt=F32):
            return ctx.enter_context(nc.sbuf_tensor(name, shape, dt))

        def psum(name, shape):
            return ctx.enter_context(nc.psum_tensor(name, shape, F32))

        def sem(name):
            return ctx.enter_context(nc.semaphore(name))

        st = psum("st", [P, 4, CHUNK])
        ring = psum("ring", [P, 2, CHUNK])
        pv = psum("pv", [P, CHUNK])
        misc = psum("misc", [P, CHUNK])
        misc_bf = misc[:, 0:64].bitcast(BF16)

        ident = sb("ident", [P, P])
        ident_bf = sb("ident_bf", [P, P], BF16)
        causal = sb("causal", [P, P])
        ones = sb("ones", [P, P])
        mhalf = sb("mhalf", [P, CT])
        prio = sb("prio", [P, EXPERTS])
        rope_sb = sb("rope_sb", [P, 2, TILES, DK])
        x_sb = sb("x_sb", [P, BATCH * TILES, D])
        wqkv = sb("wqkv", [P, 3 * D])
        wo_sb = sb("wo_sb", [P, D])
        wmod_sb = sb("wmod_sb", [P, 6 * D])
        wffn = sb("wffn", [P, EXPERTS, D])
        brow = sb("brow", [P, CT, D])
        small = sb("small", [P, D])
        cond_t = sb("cond_t", [P, BATCH])
        cond_e = sb("cond_e", [P, BATCH])
        cond_1 = sb("cond_1", [P, BATCH])
        cond_r = sb("cond_r", [P, BATCH])
        silu_t = sb("silu_t", [P, BATCH])
        silu_bc = sb("silu_bc", [P, BATCH, P])
        sig_neg = sb("sig_neg", [P, EXPERTS])
        sign_t = sb("sign_t", [P, EXPERTS])
        mod_t = sb("mod_t", [P, 4, BATCH])
        gate_raw = sb("gate_raw", [P, 2 * BATCH, D])
        gate_abs = sb("gate_abs", [P, 2 * BATCH, D])
        gate_big = sb("gate_big", [P, 2 * BATCH, D])
        gate_sg2 = sb("gate_sg2", [P, 2 * BATCH, D])
        gate_sgn = sb("gate_sgn", [P, 2 * BATCH, D])
        gate = sb("gate", [P, 2 * BATCH, D])
        wo_g = sb("wo_g", [P, BATCH, D])
        wffn_g = sb("wffn_g", [P, BATCH, EXPERTS, D])
        bias_g = sb("bias_g", [P, BATCH, CT, D])

        stats = sb("stats", [P, CT, 6])
        mv = sb("mv", [P, CT, 2])
        var_eps = sb("var_eps", [P, CT])
        rstd = sb("rstd", [P, CT])
        xh = sb("xh", [P, CT, D])
        ht = sb("ht", [P, CHUNK])
        rot_a = sb("rot_a", [P, 2, 2, 2 * D])
        rot_b = sb("rot_b", [P, 2, 2, 2 * D])
        roped = sb("roped", [P, CT, 2 * D])
        resid = sb("resid", [P, 2, CHUNK])
        parts = sb("parts", [P, 2, 2, 3, CHUNK], BF16)
        v_tok = sb("v_tok", [P, GROUPS, TILES, GH * DK])

        qs = [sb(f"qs{i}", [P, GH, SEQ], BF16) for i in range(2)]
        ks = [sb(f"ks{i}", [P, GH, SEQ], BF16) for i in range(2)]
        vg = [sb(f"vg{i}", [P, TILES, GH, VW]) for i in range(2)]
        prob = [sb(f"prob{i}", [P, GH, CHUNK]) for i in range(PRING)]
        junk = [sb(f"junk{i}", [P, P], BF16) for i in range(8)]
        pmax = sb("pmax", [P, 2, GH, CT, 4])
        rmax = [sb(f"rmax{i}", [P, GH, CT]) for i in range(2)]
        mres = [sb(f"mres{i}", [P, GH, CT]) for i in range(2)]
        msp = [sb(f"msp{i}", [P, GH, 3, CT], BF16) for i in range(2)]
        mt = [[sb(f"mt{p}{h}", [GH * 3 * CT, P], BF16) for h in range(2)] for p in range(2)]
        uo = [sb(f"uo{i}", [P, CHUNK]) for i in range(2)]
        rden = [sb(f"rden{i}", [P, CT, GH]) for i in range(2)]
        att = sb("att", [P, TILES, GROUPS, GH * DK])

        att_t = sb("att_t", [P, CHUNK])
        x2 = sb("x2", [P, CT, D])
        h2t = sb("h2t", [P, CHUNK])
        sc = sb("sc", [P, CT, EXPERTS])
        smax = sb("smax", [P, CT])
        sw = sb("sw", [P, CT, EXPERTS])
        swm = sb("swm", [P, CT])
        onehot = sb("onehot", [P, CT, 32])
        onehot_t = sb("onehot_t", [P, P])
        acc = sb("acc", [P, CT, D])
        fin = [sb(f"fin{i}", [P, CT, D]) for i in range(2)]

        x_in = [sem(f"x_in{c}") for c in range(4)]
        small_in, wmod_in, wqkv_in, rope_in = sem("small_in"), sem("wmod_in"), sem("wqkv_in"), sem("rope_in")
        late_in = sem("late_in")
        const_done = sem("const_done")
        small_full, small_read = sem("small_full"), sem("small_read")
        exp_c = sem("exp_c")
        dve_c = sem("dve_c")
        mod_full = sem("mod_full")
        gate_full = sem("gate_full")
        mod_ready = sem("mod_ready")
        gate_raw_ready = sem("gate_raw_ready")
        pool_g = sem("pool_g")
        stats_done, aggr_done, var_ready, rstd_ready = sem("stats_done"), sem("aggr_done"), sem("var_ready"), sem("rstd_ready")
        xh_ready, xt_full, ht_ready = sem("xh_ready"), sem("xt_full"), sem("ht_ready")
        qk_full, v_full, v_read, rot_ready, roped_ready = sem("qk_full"), sem("v_full"), sem("v_read"), sem("rot_ready"), sem("roped_ready")
        qkt_full, part1, res1, part2, part3 = sem("qkt_full"), sem("part1"), sem("res1"), sem("part2"), sem("part3")
        parts_out = [sem(f"parts_out{c}") for c in range(4)]
        kq_in = [[sem(f"kq_in{p}{h}") for h in range(2)] for p in range(2)]
        m_in = [[sem(f"m_in{p}{h}") for h in range(2)] for p in range(2)]
        s_full, s_free = sem("s_full"), sem("s_free")
        rmax_ready, msplit, mparts_ready = sem("rmax_ready"), sem("msplit"), sem("mparts_ready")
        mtp_full, mt_ready = sem("mtp_full"), sem("mt_ready")
        st_full, p_ready, masked, pv_done, vg_ready = sem("st_full"), sem("p_ready"), sem("masked"), sem("pv_done"), sem("vg_ready")
        u_ready, ut_full, rden_done, att_ready = sem("u_ready"), sem("ut_full"), sem("rden_done"), sem("att_ready")
        at_full, at_ready, wo_full, x2_ready = sem("at_full"), sem("at_ready"), sem("wo_full"), sem("x2_ready")
        stats2, aggr2, var2, rstd2, xh2_ready = sem("stats2"), sem("aggr2"), sem("var2"), sem("rstd2"), sem("xh2_ready")
        xt2_full, h2t_ready, sc_full, route, oh_ready = sem("xt2_full"), sem("h2t_ready"), sem("sc_full"), sem("route"), sem("oh_ready")
        oht_full, oht_ready, bias_full = sem("oht_full"), sem("oht_ready"), sem("bias_full")
        y_full, y_used, acc_step, fin_ready = sem("y_full"), sem("y_used"), sem("acc_step"), sem("fin_ready")
        out_done = [sem("out_done0"), sem("out_done1")]
        gates_ready = sem("gates_ready")

        block = ctx.enter_context(nc.Block())

        @block.sync
        def _(sp):
            for c in range(4):
                sp.dma_start(x_sb[:, CT * c:CT * c + CT, :], x_t[:, CT * c:CT * c + CT, :]).then_inc(x_in[c], 16)

            def store_parts(c):
                b = c // 2
                for ten in range(2):
                    sp.wait_ge(part3, 2 * c + ten + 1)
                    for combo in range(COMBOS):
                        part = (Q_PART, K_PART)[ten][combo]
                        sp.dma_start(
                            parts_dram[ten, HEADS * b:HEADS * b + HEADS, combo, :, CHUNK * (c % 2):CHUNK * (c % 2) + CHUNK],
                            parts[:, c % 2, ten, part, :]).then_inc(parts_out[c], 16)

            def load_stacks(a, par, hl):
                lo = CHUNK * hl
                for ten, stack in ((0, qs[par]), (1, ks[par])):
                    src = parts_dram[ten, bass.ds(GH * (2 * a + par), GH), :, :, lo:lo + CHUNK]
                    sp.dma_start(stack[0:SROWS, :, lo:lo + CHUNK], src.rearrange("h c d t -> (c d) h t")).then_inc(kq_in[par][hl], 16)

            def load_maxima(a, par, hl):
                sp.wait_ge(mt_ready, 2 * (2 * a + par) + (1 if hl else 2))
                for slot in range(GH):
                    dst = qs[par][MROW:MROW + 3, slot, CHUNK * hl:CHUNK * hl + CHUNK]
                    sp.dma_start(dst.rearrange("p (i q) -> p i q", i=CT),
                                 mt[par][hl][12 * slot:12 * slot + 12, :]).then_inc(m_in[par][hl], 16)

            for c in range(4):
                store_parts(c)
            for c in range(2):
                sp.wait_ge(parts_out[c], 16 * 2 * COMBOS)
            sp.wait_ge(const_done, 2)
            for par in range(2):
                load_stacks(0, par, 1)
                load_stacks(0, par, 0)
            for c in range(2, 4):
                sp.wait_ge(parts_out[c], 16 * 2 * COMBOS)
            load_maxima(0, 0, 1)

            def group(a, par, loads, more):
                u = 2 * a + par
                load_maxima(a, par, 0)
                if loads:
                    held_by(sp, x_in[0], 16, (st_full, 2 * NS * u + 16))
                    load_stacks(a + 1, par, 1)
                if more:
                    load_maxima(a + par, 1 - par, 1)
                if loads:
                    held_by(sp, x_in[0], 16, (st_full, 2 * NS * (u + 1)))
                    load_stacks(a + 1, par, 0)

            group(0, 0, True, True)
            with sp.Fori(0, 2) as it:
                group(it, 1, True, True)
                group(it + 1, 0, True, True)
            group(2, 1, True, True)
            group(3, 0, False, True)
            group(3, 1, False, False)
            for e in range(4):
                sp.wait_ge(fin_ready, e + 1)
                sp.dma_start(out_t[:, CT * e:CT * e + CT, :], fin[e % 2][:]).then_inc(out_done[e % 2], 16)
            for i in range(2):
                sp.wait_ge(out_done[i], 32)

        @block.tensor
        def _(pe):
            pe.wait_ge(const_done, 1)
            pe.wait_ge(small_in, 32)
            pe.transpose(ring[:, 0, 0:BATCH], small[0:BATCH, :], ident[0:BATCH, 0:BATCH])
            pe.transpose(st[:, 0, 0:EXPERTS], small[32:32 + EXPERTS, :], ident[32:32 + EXPERTS, 32:32 + EXPERTS]).then_inc(small_full, 1)

            def modulation():
                pe.wait_ge(dve_c, 8)
                pe.wait_ge(wmod_in, 16)
                for n, j in enumerate((0, 1, 3, 4)):
                    last = pe.matmul(ring[:, 0, 16 + 2 * n:18 + 2 * n], wmod_sb[:, D * j:D * j + D], silu_t[:], start=True, stop=True)
                last.then_inc(mod_full, 1)
                for b in range(BATCH):
                    for n, j in enumerate((2, 5)):
                        last = pe.matmul(ring[:, 1, D * (2 * b + n):D * (2 * b + n + 1)], silu_bc[:, b, :],
                                         wmod_sb[:, D * j:D * j + D], start=True, stop=True)
                last.then_inc(gate_full, 1)

            def x_transposes(c):
                pe.wait_ge(xh_ready, c + 1)
                pe.wait_ge(ht_ready, c)
                for t in range(CT):
                    last = pe.transpose(misc[:, P * t:P * t + P], xh[:, t, :], ident[:])
                last.then_inc(xt_full, 1)

            def projections(c):
                pe.wait_ge(ht_ready, c + 1)
                if c == 0:
                    pe.wait_ge(wqkv_in, 48)
                for t in range(CT):
                    if c >= 2:
                        pe.wait_ge(rot_ready, 2 * (c - 2) + t // 2 + 1)
                    last = pe.matmul(st[:, 2 * (c % 2) + t // 2, 2 * D * (t % 2):2 * D * (t % 2 + 1)], ht[:, P * t:P * t + P],
                                     wqkv[:, 0:2 * D], start=True, stop=True)
                    if t % 2:
                        last.then_inc(qk_full, 1)
                pe.wait_ge(v_read, c)
                for t in range(CT):
                    last = pe.matmul(pv[:, P * t:P * t + P], ht[:, P * t:P * t + P], wqkv[:, 2 * D:3 * D], start=True, stop=True)
                last.then_inc(v_full, 1)

            def qk_transposes(c):
                pe.wait_ge(roped_ready, 2 * (c + 1))
                if c == 0:
                    pe.wait_ge(gate_raw_ready, 1)
                for ten in range(2):
                    pe.wait_ge(res1, 2 * (c - 1) + ten + 1) if c else None
                    for t in range(CT):
                        last = pe.transpose(ring[:, ten, P * t:P * t + P], roped[:, t, D * ten:D * ten + D], ident[:])
                    last.then_inc(qkt_full, 1)

            modulation()
            x_transposes(0)
            projections(0)
            for c in range(4):
                if c < 3:
                    x_transposes(c + 1)
                    projections(c + 1)
                qk_transposes(c)

            def max_item(a, par, n):
                kind, half, what = ITEMS[n]
                q, k = qs[par], ks[par]
                if n == 0:
                    pe.wait_ge(kq_in[par][1], 32 * (a + 1))
                if n == NHI - 16:
                    pe.wait_ge(kq_in[par][0], 32 * (a + 1))
                pe.wait_ge(s_free, NI * (2 * a + par) + n + 1)
                bank = ring[:, n % 2, :]

                def mm(col, pair, i, j, w):
                    return pe.matmul(bank[:, col:col + P * w], q[0:ZROWS, 2 * pair + half, P * i:P * i + P],
                                     k[0:ZROWS, 2 * pair + half, P * j:P * (j + w)], start=True, stop=True)

                for pair in range(2):
                    if kind == "diag":
                        for m in range(2):
                            last = mm(P * (2 * m + pair), pair, what[0] + m, what[0] + m, 1)
                    elif kind == "wide":
                        last = mm(2 * P * pair, pair, what[0], what[1], 2)
                    elif kind == "two":
                        for m in range(2):
                            last = mm(P * (2 * m + pair), pair, what[2 * m], what[2 * m + 1], 1)
                    elif what[1] == pair:
                        last = mm(0, pair, what[0], 0, 4)
                last.then_inc(s_full, 1)

            def max_transpose(a, par, hl):
                u = 2 * a + par
                waits = [(mparts_ready, 2 * u + (1 if hl else 2))]
                if not hl:
                    waits.append((mt_ready, 2 * u + 1))
                elif not (isinstance(a, int) and u == 0):
                    waits.append((att_ready, 2 * u - 1))
                held_by(pe, const_done, 1, *waits)
                pe.transpose(misc_bf[0:GH * 3 * CT, :], msp[hl][:].rearrange("p s k i -> p (s k i)"), ident_bf[:]).then_inc(mtp_full, 1)

            def score_unit(a, par, k, pair):
                c, j = STEPS[k]
                u = 2 * a + par
                unit = 2 * k + pair
                if k == 0 and pair == 0:
                    pe.wait_ge(m_in[par][1], 64 * (a + 1))
                if k == 8 and pair == 0:
                    pe.wait_ge(m_in[par][0], 64 * (a + 1))
                pe.wait_ge(p_ready, 2 * NS * u + unit + 1)
                off = max(0, P * j - CHUNK * c)
                for half in range(2):
                    slot = 2 * pair + half
                    last = pe.matmul(st[:, 2 * (unit % 2) + half, off:CHUNK], ks[par][:, slot, P * j:P * j + P],
                                     qs[par][:, slot, CHUNK * c + off:CHUNK * (c + 1)], start=True, stop=True)
                last.then_inc(st_full, 1)

            def weighted_sum(a, par, k):
                c, j = STEPS[k]
                u = 2 * a + par
                off = max(0, P * j - CHUNK * c)
                if k == 0:
                    pe.wait_ge(vg_ready, u + 1)
                if j == 0:
                    pe.wait_ge(u_ready, 2 * u + (1 - c))
                if P * j >= CHUNK * c:
                    pe.wait_ge(masked, 8 * u + (k - 4) + 1)
                pe.wait_ge(p_ready, 2 * NS * u + 2 * k + 2 + 2)
                for s in range(GH):
                    last = pe.matmul(pv[VW * s:VW * s + VW, off:CHUNK], vg[par][:, j, s, :], prob[k % PRING][:, s, off:CHUNK],
                                     start=(j == 0), stop=(j == (7 if c else 3)))
                last.then_inc(pv_done, 1)

            def sum_transposes(u, c):
                pe.wait_ge(u_ready, 2 * u + (2 - c))
                for t in range(CT):
                    last = pe.transpose(misc[:, P * t:P * t + P], uo[c][:, P * t:P * t + P], ident[:])
                last.then_inc(ut_full, 1)

            def group(a, par, first, more):
                u = 2 * a + par
                na, npar = a + par, 1 - par
                n = 0
                for k in range(NS):
                    score_unit(a, par, k, 0)
                    share = SHARE[k] if more else 0
                    for i in range(share // 2):
                        max_item(na, npar, n)
                        n += 1
                    score_unit(a, par, k, 1)
                    if k >= 1:
                        weighted_sum(a, par, k - 1)
                    for i in range(share - share // 2):
                        max_item(na, npar, n)
                        n += 1
                    if k == 1:
                        max_transpose(a, par, 0)
                    if k == 2 and not first:
                        pe.wait_ge(mt_ready, 2 * u + 2)
                        sum_transposes(u - 1, 0)
                    if k == 9:
                        if first:
                            pe.wait_ge(mt_ready, 2 * u + 2)
                        else:
                            pe.wait_ge(att_ready, 2 * u)
                        sum_transposes(u, 1)
                    if k == 10 and more:
                        max_transpose(na, npar, 1)
                weighted_sum(a, par, NS - 1)

            pe.sem_inc(pv_done, PRING)
            pe.wait_ge(part3, 8)
            pe.wait_ge(res1, 8)
            pe.wait_ge(rot_ready, 8)
            pe.wait_ge(v_read, 4)
            for n in range(NI):
                max_item(0, 0, n)
            max_transpose(0, 0, 1)
            group(0, 0, True, True)
            with pe.Fori(0, 3) as it:
                group(it, 1, False, True)
                group(it + 1, 0, False, True)
            group(3, 1, False, False)
            pe.wait_ge(att_ready, 15)
            sum_transposes(7, 0)

            for e in range(4):
                b, cc = e // 2, e % 2
                pe.wait_ge(att_ready, 16)
                pe.wait_ge(h2t_ready, e)
                pe.wait_ge(oh_ready, e)
                for t in range(CT):
                    last = pe.transpose(st[:, 0, P * t:P * t + P],
                                        att[:, CT * cc + t, GPB * b:GPB * b + GPB, :].rearrange("p g e -> p (g e)"), ident[:])
                last.then_inc(at_full, 1)
                pe.wait_ge(at_ready, e + 1)
                pe.wait_ge(gates_ready, 1)
                for t in range(CT):
                    last = pe.matmul(st[:, 1, P * t:P * t + P], att_t[:, P * t:P * t + P], wo_g[:, b, :], start=True, stop=True)
                last.then_inc(wo_full, 1)
                pe.wait_ge(xh2_ready, e + 1)
                for t in range(CT):
                    last = pe.transpose(st[:, 2, P * t:P * t + P], xh[:, t, :], ident[:])
                last.then_inc(xt2_full, 1)
                pe.wait_ge(h2t_ready, e + 1)
                for t in range(CT):
                    last = pe.matmul(st[:, 3, EXPERTS * t:EXPERTS * (t + 1)], h2t[:, P * t:P * t + P], sign_t[:], start=True, stop=True)
                last.then_inc(sc_full, 1)

                def experts(t, hf):
                    n = 8 * e + 2 * t + hf
                    pe.wait_ge(y_used, n + 1)
                    pe.matmul(ring[:, n % 2, :], h2t[:, P * t:P * t + P],
                              wffn_g[:, b, 4 * hf:4 * hf + 4, :].rearrange("p t e -> p (t e)"), start=True, stop=True).then_inc(y_full, 1)

                experts(0, 0)
                experts(0, 1)
                pe.wait_ge(oh_ready, e + 1)
                pe.transpose(misc[:, 0:P], onehot[:].rearrange("p t e -> p (t e)"), ident[:]).then_inc(oht_full, 1)
                pe.wait_ge(oht_ready, e + 1)
                pe.matmul(pv[:], onehot_t[:], bias_g[:, b, :, :].rearrange("p t e -> p (t e)"), start=True, stop=True).then_inc(bias_full, 1)
                for t in range(1, CT):
                    experts(t, 0)
                    experts(t, 1)

        @block.scalar
        def _(act):
            act.dma_start(small[0:BATCH, :], cond).then_inc(small_in, 16)
            act.dma_start(small[32:32 + EXPERTS, :], sigs).then_inc(small_in, 16)
            act.dma_start(wmod_sb[:], wmod).then_inc(wmod_in, 16)
            for n, w in enumerate((wq, wk, wv)):
                act.dma_start(wqkv[:, D * n:D * n + D], w).then_inc(wqkv_in, 16)
            act.dma_start(rope_sb[:], rope).then_inc(rope_in, 16)
            act.dma_start(wo_sb[:], wo).then_inc(late_in, 16)
            act.dma_start(wffn[:], w_ffn.rearrange("t d e -> d t e")).then_inc(late_in, 16)
            act.wait_ge(const_done, 2)
            for t in range(CT):
                act.dma_start(brow[32 * t:32 * t + EXPERTS, t, :], b_ffn).then_inc(late_in, 16)

            act.wait_ge(dve_c, 1)
            nc.scalar.activation(cond_e[:], cond_t[:], ACT.Exp, scale=-1.0).then_inc(exp_c, 1)
            act.wait_ge(mod_ready, 1)

            def normed(c):
                b = c // 2
                act.wait_ge(xt_full, c + 1)
                if c:
                    act.wait_ge(v_full, c)
                nc.scalar.activation(ht[:], misc[:], ACT.Identity, bias=mod_t[:, 0, b:b + 1], scale=mod_t[:, 1, b:b + 1]).then_inc(ht_ready, 1)

            def copy_v(c):
                b = c // 2
                act.wait_ge(v_full, c + 1)
                nc.scalar.copy(v_tok[:, GPB * b:GPB * b + GPB, CT * (c % 2):CT * (c % 2) + CT, :].rearrange("p g t e -> p t g e"),
                               pv[:].rearrange("p (t g e) -> p t g e", t=CT, g=GPB)).then_inc(v_read, 1)

            def split(c):
                for ten in range(2):
                    act.wait_ge(qkt_full, 2 * c + ten + 1)
                    if c >= 2:
                        act.wait_ge(parts_out[c - 2], 16 * COMBOS * 2)
                    nc.scalar.copy(parts[:, c % 2, ten, 0, :], ring[:, ten, :]).then_inc(part1, 1)
                for ten in range(2):
                    act.wait_ge(res1, 2 * c + ten + 1)
                    nc.scalar.copy(parts[:, c % 2, ten, 1, :], resid[:, ten, :]).then_inc(part2, 1)

            normed(0)
            copy_v(0)
            for c in range(4):
                if c < 3:
                    normed(c + 1)
                    copy_v(c + 1)
                split(c)

            def copy_max(a, par, hl):
                u = 2 * a + par
                act.wait_ge(mtp_full, 2 * u + (1 if hl else 2))
                act.wait_ge(m_in[par][hl], 64 * a)
                nc.scalar.copy(mt[par][hl][:], misc_bf[0:GH * 3 * CT, :]).then_inc(mt_ready, 1)

            def probabilities(a, par, k):
                c, j = STEPS[k]
                u = 2 * a + par
                off = max(0, P * j - CHUNK * c)
                for pair in range(2):
                    unit = 2 * k + pair
                    if pair == 0:
                        act.wait_ge(pv_done, NS * u + k + 1)
                    act.wait_ge(st_full, 2 * NS * u + unit + 1)
                    b0 = 2 * (unit % 2)
                    nc.scalar.activation(prob[k % PRING][:, 2 * pair:2 * pair + 2, off:CHUNK], st[:, b0:b0 + 2, off:CHUNK],
                                         ACT.Exp, scale=SCALE).then_inc(p_ready, 1)

            def copy_sums(u, c, first):
                act.wait_ge(pv_done, PRING + NS * u + (8 if c else 12))
                if not first:
                    act.wait_ge(ut_full, 2 * u - (1 if c else 0))
                nc.scalar.copy(uo[c][:], pv[:]).then_inc(u_ready, 1)

            def group(a, par, first, more):
                u = 2 * a + par
                for k in range(NS):
                    probabilities(a, par, k)
                    if k == 0 and not first:
                        copy_sums(u - 1, 0, False)
                    if k == 1:
                        copy_max(a, par, 0)
                    if k == 8:
                        copy_sums(u, 1, first)
                    if k == 10 and more:
                        copy_max(a + par, 1 - par, 1)

            act.sem_inc(p_ready, 2)
            copy_max(0, 0, 1)
            group(0, 0, True, True)
            with act.Fori(0, 3) as it:
                group(it, 1, False, True)
                group(it + 1, 0, False, True)
            group(3, 1, False, False)
            copy_sums(7, 0, False)

            for e in range(4):
                b = e // 2
                act.wait_ge(at_full, e + 1)
                if e:
                    act.wait_ge(wo_full, e)
                nc.scalar.copy(att_t[:], st[:, 0, :]).then_inc(at_ready, 1)
                act.wait_ge(xt2_full, e + 1)
                if e:
                    act.wait_ge(y_full, 8 * e)
                nc.scalar.activation(h2t[:], st[:, 2, :], ACT.Identity, bias=mod_t[:, 2, b:b + 1], scale=mod_t[:, 3, b:b + 1]).then_inc(h2t_ready, 1)
                act.wait_ge(oht_full, e + 1)
                if e:
                    act.wait_ge(bias_full, e)
                nc.scalar.copy(onehot_t[:], misc[:, 0:P]).then_inc(oht_ready, 1)

        @block.vector
        def _(dve):
            dve.wait_ge(small_full, 1)
            nc.vector.tensor_copy(cond_t[:], ring[:, 0, 0:BATCH]).then_inc(dve_c, 1)
            nc.vector.tensor_scalar(sig_neg[:], st[:, 0, 0:EXPERTS], 0.0, None, ALU.is_lt).then_inc(dve_c, 1)
            dve.wait_ge(dve_c, 2)
            nc.vector.scalar_tensor_tensor(out=sign_t[:], in0=st[:, 0, 0:EXPERTS], scalar=0.0, in1=sig_neg[:],
                                           op0=ALU.is_gt, op1=ALU.subtract).then_inc(dve_c, 1)
            dve.wait_ge(exp_c, 1)
            nc.vector.tensor_scalar(cond_1[:], cond_e[:], 1.0, None, ALU.add).then_inc(dve_c, 1)
            dve.wait_ge(dve_c, 4)
            nc.vector.reciprocal(cond_r[:], cond_1[:]).then_inc(dve_c, 1)
            dve.wait_ge(dve_c, 5)
            nc.vector.tensor_tensor(silu_t[:], cond_t[:], cond_r[:], ALU.mult).then_inc(dve_c, 1)
            dve.wait_ge(dve_c, 6)
            for b in range(BATCH):
                nc.vector.tensor_scalar(silu_bc[:, b, :], ones[:], silu_t[:, b:b + 1], None, ALU.mult).then_inc(dve_c, 1)

            def norm(n, src, stat_s, aggr_s, var_s, rstd_s, out_s):
                for t in range(CT):
                    nc.vector.bn_stats(stats[:, t, :], src[:, t, :]).then_inc(stat_s, 1)
                dve.wait_ge(stat_s, CT * (n + 1))
                for t in range(CT):
                    nc.vector.bn_aggr(mv[:, t, :], stats[:, t, :]).then_inc(aggr_s, 1)
                dve.wait_ge(aggr_s, CT * (n + 1))
                nc.vector.tensor_scalar(var_eps[:], mv[:, :, 1], EPS, None, ALU.add).then_inc(var_s, 1)
                dve.wait_ge(rstd_s, n + 1)
                for t in range(CT):
                    last = nc.vector.tensor_scalar(xh[:, t, :], src[:, t, :], mv[:, t, 0:1], rstd[:, t:t + 1], ALU.subtract, ALU.mult)
                last.then_inc(out_s, 1)

            def front_norm(c):
                dve.wait_ge(x_in[c], 16)
                if c:
                    dve.wait_ge(xt_full, c)
                norm(c, x_sb[:, CT * c:CT * c + CT, :], stats_done, aggr_done, var_ready, rstd_ready, xh_ready)

            def rotate(c):
                tile0 = CT * (c % 2)
                for h in range(2):
                    dve.wait_ge(qk_full, 2 * c + h + 1)
                    if c:
                        dve.wait_ge(roped_ready, 2 * (c - 1) + h + 1)
                    bank = st[:, 2 * (c % 2) + h, :]
                    tabs = [rope_sb[:, w, tile0 + 2 * h:tile0 + 2 * h + 2, :] for w in range(2)]
                    q4 = bank.rearrange("p (t h d) -> p t h d", t=2, d=DK)
                    ob = rot_b[:, h, :, :].rearrange("p t (h d) -> p t h d", d=DK)
                    nc.vector.tensor_tensor(rot_a[:, h, :, :].rearrange("p t (h d) -> p t h d", d=DK), q4,
                                            tabs[0].rearrange("p t (o d) -> p t o d", o=1).broadcast_to([P, 2, 2 * HEADS, DK]), ALU.mult)
                    for odd in range(2):
                        last = nc.vector.tensor_tensor(
                            ob[:, :, :, odd:DK:2], q4[:, :, :, 1 - odd:DK:2],
                            tabs[1][:, :, odd:DK:2].rearrange("p t (o d) -> p t o d", o=1).broadcast_to([P, 2, 2 * HEADS, DK // 2]), ALU.mult)
                    last.then_inc(rot_ready, 1)

            def split(c):
                for ten in range(2):
                    dve.wait_ge(part1, 2 * c + ten + 1)
                    if c:
                        dve.wait_ge(part3, 2 * (c - 1) + ten + 1)
                    nc.vector.tensor_tensor(resid[:, ten, :], ring[:, ten, :], parts[:, c % 2, ten, 0, :], ALU.subtract).then_inc(res1, 1)
                for ten in range(2):
                    dve.wait_ge(part2, 2 * c + ten + 1)
                    nc.vector.tensor_tensor(parts[:, c % 2, ten, 2, :], resid[:, ten, :], parts[:, c % 2, ten, 1, :], ALU.subtract).then_inc(part3, 1)

            front_norm(0)
            dve.wait_ge(mod_full, 1)
            for n in range(4):
                last = nc.vector.tensor_scalar(mod_t[:, n, :], ring[:, 0, 16 + 2 * n:18 + 2 * n], float(n % 2), None, ALU.add)
            last.then_inc(mod_ready, 1)
            dve.wait_ge(gate_full, 1)
            nc.vector.tensor_copy(gate_raw[:].rearrange("p g d -> p (g d)"), ring[:, 1, :]).then_inc(gate_raw_ready, 1)
            front_norm(1)
            dve.wait_ge(rope_in, 16)
            rotate(0)
            for c in range(4):
                if c < 2:
                    front_norm(c + 2)
                if c < 3:
                    rotate(c + 1)
                split(c)

            def max_item(a, par, n):
                kind, half, what = ITEMS[n]
                v = 2 * a + par
                if kind == "diag":
                    held_by(dve, const_done, 2, (s_full, NI * v + n + 1), (s_free, NI * v + n + 1))
                else:
                    dve.wait_ge(s_full, NI * v + n + 1)
                bank = ring[:, n % 2, :]
                hl = 1 if n < NHI else 0
                t0 = CT * hl

                def to(i, pair, part):
                    return pmax[:, hl, 2 * pair + half, i - t0, part:part + 1]

                if kind == "diag":
                    for m in range(2):
                        for pair in range(2):
                            blk = 2 * m + pair
                            last = nc.vector.tensor_tensor_reduce(
                                out=junk[4 * (n % 2) + blk][:], in0=bank[:, P * blk:P * blk + P], in1=causal[:], scale=1.0,
                                scalar=-3.0e38, op0=ALU.add, op1=ALU.max, accum_out=to(what[0] + m, pair, 0))
                elif kind == "wide":
                    i = what[0] - t0
                    last = nc.vector.tensor_reduce(pmax[:, hl, half:GH:2, i, 1], bank.rearrange("p (a k) -> p a k", a=2), AX_X, ALU.max)
                elif kind == "two":
                    i0, i1 = what[0] - t0, what[2] - t0
                    last = nc.vector.tensor_reduce(pmax[:, hl, half:GH:2, i0:i1 + 1:i1 - i0, 2].rearrange("p s i -> p i s"),
                                                   bank.rearrange("p (i a k) -> p i a k", i=2, a=2), AX_X, ALU.max)
                else:
                    last = nc.vector.tensor_reduce(to(what[0], what[1], 3), bank, AX_X, ALU.max)
                last.then_inc(s_free, 1)

            def row_max(a, par, hl):
                v = 2 * a + par
                dve.wait_ge(s_free, 2 + NI * v + (NHI if hl else NI))
                dve.wait_ge(mparts_ready, 2 * v + (1 if hl else 2) - (1 if hl else 2) ) if isinstance(a, int) and v == 0 else \
                    dve.wait_ge(mparts_ready, 2 * (v - 1) + (1 if hl else 2))
                nc.vector.tensor_reduce(rmax[hl][:], pmax[:, hl, :, :, :], AX_X, ALU.max).then_inc(rmax_ready, 1)

            def normalise(u, c):
                dve.wait_ge(ut_full, 2 * u + (2 - c))
                sums = misc[:].rearrange("p (t s e) -> p t s e", t=CT, s=GH)
                nc.vector.reciprocal(rden[c][:], sums[:, :, :, DK]).then_inc(rden_done, 1)
                dve.wait_ge(rden_done, 2 * u + (2 - c))
                out_ap = att[:, CT * c:CT * c + CT, bass.ds(u, 1), :].rearrange("p t o e -> p t (o e)")
                nc.vector.tensor_tensor(out_ap.rearrange("p t (s d) -> p t s d", s=GH), sums[:, :, :, 0:DK],
                                        rden[c][:].rearrange("p t (s o) -> p t s o", o=1).broadcast_to([P, CT, GH, DK]), ALU.mult).then_inc(att_ready, 1)

            def group(a, par, first, more):
                u = 2 * a + par
                na, npar = a + par, 1 - par
                for n in range(NI):
                    if more:
                        max_item(na, npar, n)
                    if n == 12 and not first:
                        normalise(u - 1, 0)
                    if n == NHI - 1 and more:
                        row_max(na, npar, 1)
                    if n == 32:
                        normalise(u, 1)
                if more:
                    row_max(na, npar, 0)

            dve.sem_inc(s_free, 2)
            dve.wait_ge(const_done, 2)
            for n in range(NI):
                max_item(0, 0, n)
                if n == NHI - 1:
                    row_max(0, 0, 1)
            row_max(0, 0, 0)
            group(0, 0, True, True)
            with dve.Fori(0, 3) as it:
                group(it, 1, False, True)
                group(it + 1, 0, False, True)
            group(3, 1, False, False)
            normalise(7, 0)

            dve.sem_inc(y_used, 2)
            for e in range(4):
                dve.wait_ge(wo_full, e + 1)
                if e:
                    dve.wait_ge(acc_step, 32 * e)
                    dve.wait_ge(xt2_full, e)
                nc.vector.tensor_tensor(x2[:].rearrange("p t d -> p (t d)"), x_sb[:, CT * e:CT * e + CT, :].rearrange("p t d -> p (t d)"),
                                        st[:, 1, :], ALU.add).then_inc(x2_ready, 1)
                dve.wait_ge(x2_ready, e + 1)
                norm(e, x2, stats2, aggr2, var2, rstd2, xh2_ready)
                dve.wait_ge(sc_full, e + 1)
                sv = st[:, 3, 0:CT * EXPERTS].rearrange("p (t e) -> p t e", t=CT)
                nc.vector.tensor_reduce(smax[:], sv, AX_X, ALU.max).then_inc(route, 1)
                dve.wait_ge(route, 4 * e + 1)
                nc.vector.tensor_tensor(sc[:], sv, smax[:].rearrange("p (t o) -> p t o", o=1).broadcast_to([P, CT, EXPERTS]), ALU.is_ge).then_inc(route, 1)
                dve.wait_ge(route, 4 * e + 2)
                nc.vector.tensor_tensor(sw[:], sc[:], prio[:].rearrange("p (o e) -> p o e", o=1).broadcast_to([P, CT, EXPERTS]), ALU.mult).then_inc(route, 1)
                dve.wait_ge(route, 4 * e + 3)
                nc.vector.tensor_reduce(swm[:], sw[:], AX_X, ALU.max).then_inc(route, 1)
                dve.wait_ge(route, 4 * e + 4)
                if e:
                    dve.wait_ge(oht_full, e)
                nc.vector.tensor_tensor(onehot[:, :, 0:EXPERTS], sw[:], swm[:].rearrange("p (t o) -> p t o", o=1).broadcast_to([P, CT, EXPERTS]),
                                        ALU.is_equal).then_inc(oh_ready, 1)
                dve.wait_ge(oh_ready, e + 1)
                for t in range(CT):
                    for hf in range(2):
                        n = 8 * e + 2 * t + hf
                        dve.wait_ge(y_full, n + 1)
                        for q in range(4):
                            k = 4 * hf + q
                            step = 32 * e + 8 * t + k
                            if k:
                                dve.wait_ge(acc_step, step)
                            nc.vector.scalar_tensor_tensor(out=acc[:, t, :], in0=ring[:, n % 2, P * q:P * q + P], scalar=onehot[:, t, k:k + 1],
                                                           in1=(acc if k else x2)[:, t, :], op0=ALU.mult, op1=ALU.add).then_inc(acc_step, 1)
                        dve.wait_ge(acc_step, step + 1)
                        dve.sem_inc(y_used, 1)
                dve.wait_ge(bias_full, e + 1)
                if e >= 2:
                    dve.wait_ge(out_done[e % 2], 16)
                nc.vector.tensor_tensor(fin[e % 2][:].rearrange("p t d -> p (t d)"), acc[:].rearrange("p t d -> p (t d)"), pv[:], ALU.add).then_inc(fin_ready, 1)

        @block.gpsimd
        def _(pool):
            c_step = [0]
            own = sem("pool_own")

            def link(ins):
                c_step[0] += 1
                ins.then_inc(own, 1)
                pool.wait_ge(own, c_step[0])

            link(nc.gpsimd.memset(ones[:], 1.0))
            link(nc.gpsimd.affine_select(out=ident[:], in_=ones[:], compare_op=ALU.is_equal, fill=0.0, base=0,
                                         pattern=[[1, P]], channel_multiplier=-1))
            nc.gpsimd.tensor_copy(ident_bf[:], ident[:]).then_inc(const_done, 1)
            nc.gpsimd.memset(mhalf[:], -0.5).then_inc(own, 1)
            nc.gpsimd.memset(brow[:], 0.0).then_inc(own, 1)
            nc.gpsimd.memset(causal[:], 0.0).then_inc(own, 1)
            for k in range(EXPERTS):
                nc.gpsimd.memset(prio[:, k:k + 1], float(EXPERTS - k)).then_inc(own, 1)
            nc.gpsimd.memset(pmax[:], -3.0e38).then_inc(own, 1)
            nc.gpsimd.memset(onehot[:], 0.0).then_inc(own, 1)
            for i in range(2):
                nc.gpsimd.memset(vg[i][:], 0.0).then_inc(own, 1)
            c_step[0] += 7 + EXPERTS
            pool.wait_ge(own, c_step[0])
            for i in range(2):
                for stack, value in ((qs[i], 0.0), (ks[i], -1.0)):
                    link(nc.gpsimd.memset(stack[32:64, :, :], 0.0))
                    link(nc.gpsimd.memset(stack[64:96, :, :], 0.0))
                    link(nc.gpsimd.memset(stack[96:128, :, :], value))
            link(nc.gpsimd.affine_select(out=causal[:], in_=causal[:], compare_op=ALU.is_ge, fill=NEG, base=0,
                                         pattern=[[-1, P]], channel_multiplier=1))
            nc.gpsimd.memset(vg[0][:, :, :, DK:DK + 1], 1.0).then_inc(own, 1)
            nc.gpsimd.memset(vg[1][:, :, :, DK:DK + 1], 1.0).then_inc(own, 1)
            c_step[0] += 2
            pool.wait_ge(own, c_step[0])
            pool.sem_inc(const_done, 1)

            def power(var_s, rstd_s, n):
                pool.wait_ge(var_s, n + 1)
                nc.gpsimd.tensor_tensor(rstd[:], var_eps[:], mhalf[:], ALU.pow).then_inc(rstd_s, 1)

            def add_rotated(c):
                if c:
                    pool.wait_ge(qkt_full, 2 * c)
                for h in range(2):
                    pool.wait_ge(rot_ready, 2 * c + h + 1)
                    nc.gpsimd.tensor_tensor(roped[:, 2 * h:2 * h + 2, :], rot_a[:, h, :, :], rot_b[:, h, :, :], ALU.add).then_inc(roped_ready, 1)

            power(var_ready, rstd_ready, 0)
            power(var_ready, rstd_ready, 1)
            add_rotated(0)
            for c in range(1, 4):
                if c < 3:
                    power(var_ready, rstd_ready, c + 1)
                add_rotated(c)

            pool.wait_ge(gate_raw_ready, 1)
            nc.gpsimd.tensor_scalar(gate_sg2[:], gate_raw[:], 0.0, 2.0, ALU.is_ge, ALU.mult).then_inc(pool_g, 1)
            pool.wait_ge(pool_g, 1)
            nc.gpsimd.tensor_scalar(gate_sgn[:], gate_sg2[:], -1.0, None, ALU.add).then_inc(pool_g, 1)
            pool.wait_ge(pool_g, 2)
            nc.gpsimd.tensor_tensor(gate_abs[:], gate_raw[:], gate_sgn[:], ALU.mult).then_inc(pool_g, 1)
            pool.wait_ge(pool_g, 3)
            nc.gpsimd.tensor_scalar(gate_big[:], gate_abs[:], 0.25, None, ALU.max).then_inc(pool_g, 1)
            pool.wait_ge(pool_g, 4)
            nc.gpsimd.tensor_tensor(gate[:], gate_big[:], gate_sgn[:], ALU.mult).then_inc(pool_g, 1)
            pool.wait_ge(pool_g, 5)
            pool.wait_ge(late_in, 16 * (2 + CT))
            pool.wait_ge(const_done, 2)

            def copy_v(u, par):
                held_by(pool, v_read, 4, *([] if isinstance(u, int) and u < 2 else [(pv_done, PRING + NS * (u - 1))]))
                src = v_tok[:, u, :, :] if isinstance(u, int) else v_tok[:, bass.ds(u, 1), :, :].rearrange("p o t e -> p (o t) e")
                nc.gpsimd.tensor_copy(vg[par][:, :, :, 0:DK], src.rearrange("p t (s d) -> p t s d", s=GH)).then_inc(vg_ready, 1)

            copy_v(0, 0)

            def split_max(a, par, hl):
                u = 2 * a + par
                n = 2 * u + (0 if hl else 1)
                held_by(pool, const_done, 2, (rmax_ready, n + 1), *([] if isinstance(n, int) and n < 2 else [(mtp_full, n - 1)]))
                nc.gpsimd.tensor_copy(msp[hl][:, :, 0, :], rmax[hl][:]).then_inc(msplit, 1)
                pool.wait_ge(msplit, 3 * n + 1)
                nc.gpsimd.tensor_tensor(mres[hl][:], rmax[hl][:], msp[hl][:, :, 0, :], ALU.subtract).then_inc(msplit, 1)
                held_by(pool, const_done, 2, (msplit, 3 * n + 2))
                nc.gpsimd.tensor_copy(msp[hl][:, :, 1, :], mres[hl][:]).then_inc(msplit, 1)
                pool.wait_ge(msplit, 3 * n + 3)
                nc.gpsimd.tensor_tensor(msp[hl][:, :, 2, :], mres[hl][:], msp[hl][:, :, 1, :], ALU.subtract).then_inc(mparts_ready, 1)

            def mask(a, par, k):
                c, j = STEPS[k]
                off = P * j - CHUNK * c
                held_by(pool, const_done, 2, (p_ready, 2 * NS * (2 * a + par) + 2 * k + 2 + 2))
                d = prob[k % PRING][:, :, off:off + P]
                nc.gpsimd.affine_select(out=d, in_=d, compare_op=ALU.is_ge, fill=0.0, base=0,
                                        pattern=[[0, GH], [1, P]], channel_multiplier=-1).then_inc(masked, 1)

            def group(a, par, first, more):
                u = 2 * a + par
                if not first:
                    split_max(a, par, 0)
                if more:
                    copy_v(u + 1, 1 - par)
                for k in range(4, NS):
                    mask(a, par, k)
                    if k == 6 and more:
                        split_max(a + par, 1 - par, 1)

            split_max(0, 0, 1)
            split_max(0, 0, 0)
            for b in range(BATCH):
                nc.gpsimd.tensor_tensor(wo_g[:, b, :], wo_sb[:], gate[:, 2 * b, :], ALU.mult).then_inc(pool_g, 1)
                gb = gate[:, 2 * b + 1, :].rearrange("p (o d) -> p o d", o=1)
                nc.gpsimd.tensor_tensor(wffn_g[:, b, :, :], wffn[:], gb.broadcast_to([P, EXPERTS, D]), ALU.mult).then_inc(pool_g, 1)
                nc.gpsimd.tensor_tensor(bias_g[:, b, :, :], brow[:], gb.broadcast_to([P, CT, D]), ALU.mult).then_inc(pool_g, 1)
            pool.wait_ge(pool_g, 11)
            pool.sem_inc(gates_ready, 1)
            group(0, 0, True, True)
            with pool.Fori(0, 3) as it:
                group(it, 1, False, True)
                group(it + 1, 0, False, True)
            group(3, 1, False, False)
            for e in range(4):
                power(var2, rstd2, e)


_INS = ["L0_attn_x", "L0_attn_Wq", "L0_attn_Wk", "L0_attn_Wv", "L0_attn_Wo", "L0_ffn_tile_sigs", "L0_ffn_W", "L0_ffn_b",
        "L0_c", "L0_wmod"]


def kernel(**inputs):
    import concourse.bacc as bacc
    from concourse.bass_utils import run_bass_kernel_spmd

    nc = bacc.Bacc("TRN2", target_bir_lowering=False, num_devices=1)
    arrays, args = {}, []
    for name in _INS:
        a = np.ascontiguousarray(inputs[name])
        arrays[f"in_{name}"] = a
        args.append(nc.dram_tensor(f"in_{name}", a.shape, mybir.dt.from_np(a.dtype), kind="ExternalInput").ap())
    tables = rope_tables()
    arrays["in_rope"] = tables
    args.append(nc.dram_tensor("in_rope", tables.shape, F32, kind="ExternalInput").ap())
    out = nc.dram_tensor("out_x", (BATCH, SEQ, D), F32, kind="ExternalOutput").ap()
    adaln_block_kernel(nc, *args, out)
    r = run_bass_kernel_spmd(nc, [arrays], core_ids=[0])
    return r.results[0]["out_x"]
```

```python
from contextlib import ExitStack

import numpy as np

import concourse.bass as bass
from concourse import mybir

F32 = mybir.dt.float32
BF16 = mybir.dt.bfloat16
ALU = mybir.AluOpType
ACT = mybir.ActivationFunctionType
AX_X = mybir.AxisListType.X

P = 128
BATCH, SEQ, D = 2, 1024, 128
HEADS = 16
DK = D // HEADS
EXPERTS = 8
TILES = SEQ // P
CHUNK = 512
CT = CHUNK // P
GH = 4
GROUPS = BATCH * HEADS // GH
GPB = HEADS // GH
SCALE = float(DK) ** -0.5
EPS = 1e-5
COMBOS = 6
TAKEN_BY = ((slice(0, 3), slice(3, 6, 2), slice(4, 5)), (slice(2, 5), slice(0, 6, 5), slice(1, 2)))
SROWS = COMBOS * DK
ZROWS = 96
MROW = ZROWS
VW = 32
NEG = -1.0e30



def max_items():
    hi = [("diag", h, (i,)) for i in (4, 6) for h in (0, 1)]
    hi += [("wide", h, (6, 4)) for h in (0, 1)] + [("wide", h, (7, 5)) for h in (0, 1)]
    hi += [("two", h, (5, 4, 7, 4)) for h in (0, 1)]
    hi += [("full", h, (i, pr)) for i in range(4, 8) for pr in (0, 1) for h in (0, 1)]
    lo = [("diag", h, (i,)) for i in (0, 2) for h in (0, 1)]
    lo += [("wide", h, (2, 0)) for h in (0, 1)] + [("wide", h, (3, 1)) for h in (0, 1)]
    lo += [("two", h, (1, 0, 3, 0)) for h in (0, 1)]
    return hi, lo


HI, LO = max_items()
ITEMS = HI + LO
NI, NHI = len(ITEMS), len(HI)

STEPS = [(1, j) for j in range(8)] + [(0, j) for j in range(4)]
NS = len(STEPS)
PRING = 3
SHARE = [(2, 1, 1, 1), (0, 1, 2, 1), (0, 1, 2, 1), (0, 1, 2, 1), (0, 1, 1, 1), (0, 1, 1, 1), (0, 1, 1, 1), (0, 1, 1, 0),
         (0, 1, 1, 0), (0, 1, 1, 0), (0, 1, 1, 0), (0, 1, 1, 0)]
assert sum(map(sum, SHARE)) == NI and NS % PRING == 0
NORM_AT = sum(map(sum, SHARE[:4]))
LAG = 2


def held_by(engine, always, count, *waits):
    counts = [(s, n if isinstance(n, int) else engine.to_reg(n)) for s, n in waits]
    engine.wait_ge(always, count)
    for s, n in counts:
        engine.wait_ge(s, n)


def rope_tables():
    inv = (1.0 / np.float32(10000.0) ** (np.arange(0, DK, 2, dtype=np.float32) / np.float32(DK))).astype(np.float32)
    ang = np.outer(np.arange(SEQ, dtype=np.float32), inv).astype(np.float32)
    cos = np.repeat(np.cos(ang), 2, axis=-1)
    sin = np.repeat(np.sin(ang), 2, axis=-1)
    sin[:, 0::2] *= -1.0
    both = np.stack([cos, sin]).astype(np.float32).reshape(2, TILES, P, DK)
    return np.ascontiguousarray(both.transpose(2, 0, 1, 3))


def adaln_block_kernel(nc, x, wq, wk, wv, wo, sigs, w_ffn, b_ffn, cond, wmod, rope, out):
    x_t = x.rearrange("b (t p) d -> p (b t) d", p=P)
    out_t = out.rearrange("b (t p) d -> p (b t) d", p=P)
    parts_dram = nc.dram_tensor("parts_dram", (2, GROUPS * GH, DK, COMBOS, SEQ), BF16).ap()

    with ExitStack() as ctx:
        def sb(name, shape, dt=F32):
            return ctx.enter_context(nc.sbuf_tensor(name, shape, dt))

        def psum(name, shape):
            return ctx.enter_context(nc.psum_tensor(name, shape, F32))

        def sem(name):
            return ctx.enter_context(nc.semaphore(name))

        st = psum("st", [P, 4, CHUNK])
        ring = psum("ring", [P, 2, CHUNK])
        pv = psum("pv", [P, CHUNK])
        misc = psum("misc", [P, CHUNK])
        misc_bf = misc[:, 0:64].bitcast(BF16)

        ident = sb("ident", [P, P])
        ident_bf = sb("ident_bf", [P, P], BF16)
        causal = sb("causal", [P, P])
        causal_bf = sb("causal_bf", [P, 4, P], BF16)
        ones = sb("ones", [P, P])
        mhalf = sb("mhalf", [P, CT])
        prio = sb("prio", [P, EXPERTS])
        rope_sb = sb("rope_sb", [P, 2, TILES, DK])
        x_sb = sb("x_sb", [P, BATCH * TILES, D])
        wqkv = sb("wqkv", [P, 3 * D])
        wo_sb = sb("wo_sb", [P, D])
        wmod_sb = sb("wmod_sb", [P, 6 * D])
        wffn = sb("wffn", [P, EXPERTS, D])
        brow = sb("brow", [P, CT, D])
        small = sb("small", [P, D])
        cond_t = sb("cond_t", [P, BATCH])
        cond_e = sb("cond_e", [P, BATCH])
        cond_1 = sb("cond_1", [P, BATCH])
        cond_r = sb("cond_r", [P, BATCH])
        silu_t = sb("silu_t", [P, BATCH])
        silu_bc = sb("silu_bc", [P, BATCH, P])
        sig_neg = sb("sig_neg", [P, EXPERTS])
        sign_t = sb("sign_t", [P, EXPERTS])
        mod_t = sb("mod_t", [P, 4, BATCH])
        gate_raw = sb("gate_raw", [P, 2 * BATCH, D])
        gate_abs = sb("gate_abs", [P, 2 * BATCH, D])
        gate_big = sb("gate_big", [P, 2 * BATCH, D])
        gate_sg2 = sb("gate_sg2", [P, 2 * BATCH, D])
        gate_sgn = sb("gate_sgn", [P, 2 * BATCH, D])
        gate = sb("gate", [P, 2 * BATCH, D])
        wo_g = sb("wo_g", [P, BATCH, D])
        wffn_g = sb("wffn_g", [P, BATCH, EXPERTS, D])
        bias_g = sb("bias_g", [P, BATCH, CT, D])

        stats = sb("stats", [P, CT, 6])
        mv = sb("mv", [P, CT, 2])
        var_eps = sb("var_eps", [P, CT])
        rstd = sb("rstd", [P, CT])
        xh = sb("xh", [P, CT, D])
        ht = sb("ht", [P, CHUNK])
        rot_a = sb("rot_a", [P, 2, 2, 2 * D])
        rot_b = sb("rot_b", [P, 2, 2, 2 * D])
        roped = sb("roped", [P, CT, 2 * D])
        resid = sb("resid", [P, 2, CHUNK])
        parts = sb("parts", [P, 2, 2, 3, CHUNK], BF16)
        v_tok = sb("v_tok", [P, GROUPS, TILES, GH * DK])

        qs = [sb(f"qs{i}", [P, 2, GH, CHUNK], BF16) for i in range(2)]
        ks = [sb(f"ks{i}", [P, 2, GH, CHUNK], BF16) for i in range(2)]
        vg = [sb(f"vg{i}", [P, TILES, GH, VW]) for i in range(2)]
        prob = [sb(f"prob{i}", [P, GH, CHUNK]) for i in range(PRING)]
        pmax = sb("pmax", [P, 2, GH, CT, 4])
        rmax = [sb(f"rmax{i}", [P, GH, CT]) for i in range(2)]
        mres = [sb(f"mres{i}", [P, GH, CT]) for i in range(2)]
        msp = [sb(f"msp{i}", [P, 3, GH, CT], BF16) for i in range(2)]
        mt = [[sb(f"mt{p}{h}", [GH * 3 * CT, P], BF16) for h in range(2)] for p in range(2)]
        uo = [sb(f"uo{i}", [P, CHUNK]) for i in range(2)]
        rden = [sb(f"rden{i}", [P, CT, GH]) for i in range(2)]
        att = sb("att", [P, TILES, GROUPS, GH * DK])

        att_t = sb("att_t", [P, CHUNK])
        x2 = sb("x2", [P, CT, D])
        h2t = sb("h2t", [P, CHUNK])
        sc = sb("sc", [P, CT, EXPERTS])
        smax = sb("smax", [P, CT])
        sw = sb("sw", [P, CT, EXPERTS])
        swm = sb("swm", [P, CT])
        onehot = sb("onehot", [P, CT, 32])
        onehot_t = sb("onehot_t", [P, P])
        acc = sb("acc", [P, CT, D])
        fin = [sb(f"fin{i}", [P, CT, D]) for i in range(2)]

        x_in = [sem(f"x_in{c}") for c in range(4)]
        small_in, wmod_in, wqkv_in, rope_in = sem("small_in"), sem("wmod_in"), sem("wqkv_in"), sem("rope_in")
        late_in = sem("late_in")
        const_done = sem("const_done")
        brow_clear = sem("brow_clear")
        small_full, small_read = sem("small_full"), sem("small_read")
        exp_c = sem("exp_c")
        dve_c = sem("dve_c")
        mod_full = sem("mod_full")
        gate_full = sem("gate_full")
        mod_ready = sem("mod_ready")
        gate_raw_ready = sem("gate_raw_ready")
        pool_g = sem("pool_g")
        stats_done, aggr_done, var_ready, rstd_ready = sem("stats_done"), sem("aggr_done"), sem("var_ready"), sem("rstd_ready")
        xh_ready, xt_full, ht_ready = sem("xh_ready"), sem("xt_full"), sem("ht_ready")
        qk_full, v_full, v_read, rot_ready, roped_ready = sem("qk_full"), sem("v_full"), sem("v_read"), sem("rot_ready"), sem("roped_ready")
        qkt_full, part1, res1, part2, part3 = sem("qkt_full"), sem("part1"), sem("res1"), sem("part2"), sem("part3")
        parts_out = [sem(f"parts_out{c}") for c in range(4)]
        kq_in = [[sem(f"kq_in{p}{h}") for h in range(2)] for p in range(2)]
        m_in = [[sem(f"m_in{p}{h}") for h in range(2)] for p in range(2)]
        s_full, s_free = sem("s_full"), sem("s_free")
        rmax_ready, msplit, mparts_ready = sem("rmax_ready"), sem("msplit"), sem("mparts_ready")
        mtp_full, mt_ready = sem("mtp_full"), sem("mt_ready")
        st_full, p_ready, masked, pv_done, vg_ready = sem("st_full"), sem("p_ready"), sem("masked"), sem("pv_done"), sem("vg_ready")
        u_ready, ut_full, rden_done, att_ready = sem("u_ready"), sem("ut_full"), sem("rden_done"), sem("att_ready")
        at_full, at_ready, wo_full, x2_ready = sem("at_full"), sem("at_ready"), sem("wo_full"), sem("x2_ready")
        stats2, aggr2, var2, rstd2, xh2_ready = sem("stats2"), sem("aggr2"), sem("var2"), sem("rstd2"), sem("xh2_ready")
        xt2_full, h2t_ready, sc_full, route, oh_ready = sem("xt2_full"), sem("h2t_ready"), sem("sc_full"), sem("route"), sem("oh_ready")
        oht_full, oht_ready, bias_full = sem("oht_full"), sem("oht_ready"), sem("bias_full")
        y_full, y_used, acc_step, fin_ready = sem("y_full"), sem("y_used"), sem("acc_step"), sem("fin_ready")
        out_done = [sem("out_done0"), sem("out_done1")]
        gates_ready = sem("gates_ready")

        block = ctx.enter_context(nc.Block())

        @block.sync
        def _(sp):
            for c in range(4):
                sp.dma_start(x_sb[:, CT * c:CT * c + CT, :], x_t[:, CT * c:CT * c + CT, :]).then_inc(x_in[c], 16)

            def store_parts(c):
                b = c // 2
                for ten in range(2):
                    sp.wait_ge(part3, 2 * c + ten + 1)
                    for part in range(3):
                        dst = parts_dram[ten, HEADS * b:HEADS * b + HEADS, :, TAKEN_BY[ten][part], CHUNK * (c % 2):CHUNK * (c % 2) + CHUNK]
                        src = parts[:, c % 2, ten, part, :].rearrange("p (o t) -> p o t", o=1)
                        sp.dma_start(dst.rearrange("h d c t -> (h d) c t"),
                                     src.broadcast_to([P, (3, 2, 1)[part], CHUNK])).then_inc(parts_out[c], 16)

            def load_stacks(a, par, hl):
                lo = CHUNK * hl
                for ten, stack in ((0, qs[par]), (1, ks[par])):
                    src = parts_dram[ten, bass.ds(GH * (2 * a + par), GH), :, :, lo:lo + CHUNK]
                    sp.dma_start(stack[0:SROWS, hl, :, :], src.rearrange("h d c t -> (d c) h t")).then_inc(kq_in[par][hl], 16)

            def load_maxima(a, par, hl):
                sp.wait_ge(mt_ready, 2 * (2 * a + par) + (1 if hl else 2))
                sp.dma_start(qs[par][MROW:MROW + 3, hl, :, :], mt[par][hl][:]).then_inc(m_in[par][hl], 16)

            for c in range(2):
                store_parts(c)
            for c in range(2):
                sp.wait_ge(parts_out[c], 16 * 6)
            sp.wait_ge(const_done, 2)
            for par in range(2):
                load_stacks(0, par, 1)
                load_stacks(0, par, 0)
            for c in range(2, 4):
                store_parts(c)
            load_maxima(0, 0, 1)
            for c in range(2, 4):
                sp.wait_ge(parts_out[c], 16 * 6)

            def group(a, par, loads, more):
                u = 2 * a + par
                load_maxima(a, par, 0)
                if loads:
                    held_by(sp, x_in[0], 16, (st_full, 2 * NS * u + 16))
                    load_stacks(a + 1, par, 1)
                if more:
                    load_maxima(a + par, 1 - par, 1)
                if loads:
                    held_by(sp, x_in[0], 16, (st_full, 2 * NS * (u + 1)))
                    load_stacks(a + 1, par, 0)

            group(0, 0, True, True)
            with sp.Fori(0, 2) as it:
                group(it, 1, True, True)
                group(it + 1, 0, True, True)
            group(2, 1, True, True)
            group(3, 0, False, True)
            group(3, 1, False, False)
            for e in range(4):
                sp.wait_ge(fin_ready, e + 1)
                sp.dma_start(out_t[:, CT * e:CT * e + CT, :], fin[e % 2][:]).then_inc(out_done[e % 2], 16)
            for i in range(2):
                sp.wait_ge(out_done[i], 32)

        @block.tensor
        def _(pe):
            pe.wait_ge(const_done, 1)
            pe.wait_ge(small_in, 32)
            pe.transpose(ring[:, 0, 0:BATCH], small[0:BATCH, :], ident[0:BATCH, 0:BATCH])
            pe.transpose(st[:, 0, 0:EXPERTS], small[32:32 + EXPERTS, :], ident[32:32 + EXPERTS, 32:32 + EXPERTS]).then_inc(small_full, 1)

            def modulation():
                pe.wait_ge(dve_c, 8)
                pe.wait_ge(wmod_in, 16)
                for n, j in enumerate((0, 1, 3, 4)):
                    last = pe.matmul(ring[:, 0, 16 + 2 * n:18 + 2 * n], wmod_sb[:, D * j:D * j + D], silu_t[:], start=True, stop=True)
                last.then_inc(mod_full, 1)
                for b in range(BATCH):
                    for n, j in enumerate((2, 5)):
                        last = pe.matmul(ring[:, 1, D * (2 * b + n):D * (2 * b + n + 1)], silu_bc[:, b, :],
                                         wmod_sb[:, D * j:D * j + D], start=True, stop=True)
                last.then_inc(gate_full, 1)

            def x_transposes(c):
                pe.wait_ge(xh_ready, c + 1)
                pe.wait_ge(ht_ready, c)
                for t in range(CT):
                    last = pe.transpose(misc[:, P * t:P * t + P], xh[:, t, :], ident[:])
                last.then_inc(xt_full, 1)

            def projections(c):
                pe.wait_ge(ht_ready, c + 1)
                if c == 0:
                    pe.wait_ge(wqkv_in, 48)
                for t in range(CT):
                    if c >= 2:
                        pe.wait_ge(rot_ready, 2 * (c - 2) + t // 2 + 1)
                    last = pe.matmul(st[:, 2 * (c % 2) + t // 2, 2 * D * (t % 2):2 * D * (t % 2 + 1)], ht[:, P * t:P * t + P],
                                     wqkv[:, 0:2 * D], start=True, stop=True)
                    if t % 2:
                        last.then_inc(qk_full, 1)
                pe.wait_ge(v_read, c)
                for t in range(CT):
                    last = pe.matmul(pv[:, P * t:P * t + P], ht[:, P * t:P * t + P], wqkv[:, 2 * D:3 * D], start=True, stop=True)
                last.then_inc(v_full, 1)

            def qk_transposes(c):
                pe.wait_ge(roped_ready, 2 * (c + 1))
                if c == 0:
                    pe.wait_ge(gate_raw_ready, 1)
                for ten in range(2):
                    pe.wait_ge(res1, 2 * (c - 1) + ten + 1) if c else None
                    for t in range(CT):
                        last = pe.transpose(ring[:, ten, P * t:P * t + P], roped[:, t, D * ten:D * ten + D], ident[:])
                    last.then_inc(qkt_full, 1)

            modulation()
            x_transposes(0)
            projections(0)
            for c in range(4):
                if c < 3:
                    x_transposes(c + 1)
                    projections(c + 1)
                qk_transposes(c)

            def max_item(a, par, n):
                kind, half, what = ITEMS[n]
                q, k = qs[par], ks[par]
                if n == 0:
                    pe.wait_ge(kq_in[par][1], 32 * (a + 1))
                if n == NHI - 16:
                    pe.wait_ge(kq_in[par][0], 32 * (a + 1))
                pe.wait_ge(s_free, NI * (2 * a + par) + n + 1)
                bank = ring[:, n % 2, :]

                def mm(col, pair, i, j, w, start=True, stop=True):
                    return pe.matmul(bank[:, col:col + P * w], q[0:ZROWS, i // CT, 2 * pair + half, P * (i % CT):P * (i % CT) + P],
                                     k[0:ZROWS, j // CT, 2 * pair + half, P * (j % CT):P * (j % CT + w)], start=start, stop=stop)

                if kind == "diag":
                    pe.matmul(bank, ident_bf[:], causal_bf[:].rearrange("p m k -> p (m k)"), start=True, stop=False)
                for pair in range(2):
                    if kind == "diag":
                        for m in range(2):
                            last = mm(P * (2 * m + pair), pair, what[0] + m, what[0] + m, 1, start=False, stop=(pair == 1 and m == 1))
                    elif kind == "wide":
                        last = mm(2 * P * pair, pair, what[0], what[1], 2)
                    elif kind == "two":
                        for m in range(2):
                            last = mm(P * (2 * m + pair), pair, what[2 * m], what[2 * m + 1], 1)
                    elif what[1] == pair:
                        last = mm(0, pair, what[0], 0, 4)
                last.then_inc(s_full, 1)

            def max_transpose(a, par, hl):
                u = 2 * a + par
                waits = [(mparts_ready, 2 * u + (1 if hl else 2))]
                if isinstance(u, int) and u < 2 and (hl or u == 0):
                    if u or not hl:
                        waits.append((mt_ready, 2 if hl else 1))
                else:
                    waits.append((att_ready, 2 * u - (2 if hl else 1)))
                held_by(pe, const_done, 1, *waits)
                pe.transpose(misc_bf[0:GH * 3 * CT, :], msp[hl][:].rearrange("p k s i -> p (k s i)"), ident_bf[:]).then_inc(mtp_full, 1)

            def score_unit(a, par, k, pair):
                c, j = STEPS[k]
                u = 2 * a + par
                unit = 2 * k + pair
                if k == 0 and pair == 0:
                    pe.wait_ge(m_in[par][1], 16 * (a + 1))
                if k == 8 and pair == 0:
                    pe.wait_ge(m_in[par][0], 16 * (a + 1))
                pe.wait_ge(p_ready, 2 * NS * u + unit + 1)
                off = max(0, P * j - CHUNK * c)
                for half in range(2):
                    slot = 2 * pair + half
                    last = pe.matmul(st[:, 2 * (unit % 2) + half, off:CHUNK], ks[par][:, j // CT, slot, P * (j % CT):P * (j % CT) + P],
                                     qs[par][:, c, slot, off:CHUNK], start=True, stop=True)
                last.then_inc(st_full, 1)

            def weighted_sum(a, par, k):
                c, j = STEPS[k]
                u = 2 * a + par
                off = max(0, P * j - CHUNK * c)
                if k == 0:
                    pe.wait_ge(vg_ready, u + 1)
                if j == 0:
                    pe.wait_ge(u_ready, 2 * u + (1 - c))
                if P * j >= CHUNK * c:
                    pe.wait_ge(masked, 8 * u + (k - 4) + 1)
                pe.wait_ge(p_ready, 2 * NS * u + 2 * k + 2 + 2)
                for s in range(GH):
                    last = pe.matmul(pv[VW * s:VW * s + VW, off:CHUNK], vg[par][:, j, s, :], prob[k % PRING][:, s, off:CHUNK],
                                     start=(j == 0), stop=(j == (7 if c else 3)))
                last.then_inc(pv_done, 1)

            def sum_transposes(u, c):
                pe.wait_ge(u_ready, 2 * u + (2 - c))
                for t in range(CT):
                    last = pe.transpose(misc[:, P * t:P * t + P], uo[c][:, P * t:P * t + P], ident[:])
                last.then_inc(ut_full, 1)

            def group(a, par, first, more):
                u = 2 * a + par
                na, npar = a + par, 1 - par
                n = 0

                def items(count):
                    nonlocal n
                    for _ in range(count if more else 0):
                        max_item(na, npar, n)
                        n += 1

                for k in range(NS):
                    items(SHARE[k][0])
                    score_unit(a, par, k, 0)
                    items(SHARE[k][1])
                    if k >= LAG:
                        weighted_sum(a, par, k - LAG)
                    elif not first:
                        weighted_sum(a + par - 1, 1 - par, NS + k - LAG)
                    items(SHARE[k][2])
                    score_unit(a, par, k, 1)
                    items(SHARE[k][3])
                    if k == 1:
                        max_transpose(a, par, 0)
                    if k == 3 and not first:
                        pe.wait_ge(mt_ready, 2 * u + 2)
                        sum_transposes(u - 1, 0)
                    if k == 9 and more:
                        max_transpose(na, npar, 1)
                    if k == 11:
                        pe.wait_ge(*((mt_ready, 2 * u + 3) if more else (att_ready, 2 * u)))
                        sum_transposes(u, 1)

            pe.sem_inc(pv_done, PRING)
            pe.wait_ge(part3, 8)
            pe.wait_ge(res1, 8)
            pe.wait_ge(rot_ready, 8)
            pe.wait_ge(v_read, 4)
            pe.wait_ge(const_done, 2)
            for n in range(NI):
                max_item(0, 0, n)
            max_transpose(0, 0, 1)
            group(0, 0, True, True)
            with pe.Fori(0, 3) as it:
                group(it, 1, False, True)
                group(it + 1, 0, False, True)
            group(3, 1, False, False)
            for k in range(NS - LAG, NS):
                weighted_sum(3, 1, k)
            pe.wait_ge(att_ready, 15)
            sum_transposes(7, 0)

            for e in range(4):
                b, cc = e // 2, e % 2
                pe.wait_ge(att_ready, 16)
                pe.wait_ge(h2t_ready, e)
                pe.wait_ge(oh_ready, e)
                for t in range(CT):
                    last = pe.transpose(st[:, 0, P * t:P * t + P],
                                        att[:, CT * cc + t, GPB * b:GPB * b + GPB, :].rearrange("p g e -> p (g e)"), ident[:])
                last.then_inc(at_full, 1)
                pe.wait_ge(at_ready, e + 1)
                pe.wait_ge(gates_ready, 1)
                for t in range(CT):
                    last = pe.matmul(st[:, 1, P * t:P * t + P], att_t[:, P * t:P * t + P], wo_g[:, b, :], start=True, stop=True)
                last.then_inc(wo_full, 1)
                pe.wait_ge(xh2_ready, e + 1)
                for t in range(CT):
                    last = pe.transpose(st[:, 2, P * t:P * t + P], xh[:, t, :], ident[:])
                last.then_inc(xt2_full, 1)
                pe.wait_ge(h2t_ready, e + 1)
                for t in range(CT):
                    last = pe.matmul(st[:, 3, EXPERTS * t:EXPERTS * (t + 1)], h2t[:, P * t:P * t + P], sign_t[:], start=True, stop=True)
                last.then_inc(sc_full, 1)

                def experts(t, hf):
                    n = 8 * e + 2 * t + hf
                    pe.wait_ge(y_used, n + 1)
                    pe.matmul(ring[:, n % 2, :], h2t[:, P * t:P * t + P],
                              wffn_g[:, b, 4 * hf:4 * hf + 4, :].rearrange("p t e -> p (t e)"), start=True, stop=True).then_inc(y_full, 1)

                experts(0, 0)
                experts(0, 1)
                pe.wait_ge(oh_ready, e + 1)
                pe.transpose(misc[:, 0:P], onehot[:].rearrange("p t e -> p (t e)"), ident[:]).then_inc(oht_full, 1)
                pe.wait_ge(oht_ready, e + 1)
                pe.matmul(pv[:], onehot_t[:], bias_g[:, b, :, :].rearrange("p t e -> p (t e)"), start=True, stop=True).then_inc(bias_full, 1)
                for t in range(1, CT):
                    experts(t, 0)
                    experts(t, 1)

        @block.scalar
        def _(act):
            act.dma_start(small[0:BATCH, :], cond).then_inc(small_in, 16)
            act.dma_start(small[32:32 + EXPERTS, :], sigs).then_inc(small_in, 16)
            act.dma_start(wmod_sb[:], wmod).then_inc(wmod_in, 16)
            for n, w in enumerate((wq, wk, wv)):
                act.dma_start(wqkv[:, D * n:D * n + D], w).then_inc(wqkv_in, 16)
            act.dma_start(rope_sb[:], rope).then_inc(rope_in, 16)
            act.dma_start(wo_sb[:], wo).then_inc(late_in, 16)
            act.dma_start(wffn[:], w_ffn.rearrange("t d e -> d t e")).then_inc(late_in, 16)
            act.wait_ge(dve_c, 1)
            nc.scalar.activation(cond_e[:], cond_t[:], ACT.Exp, scale=-1.0).then_inc(exp_c, 1)
            act.wait_ge(mod_ready, 1)

            def normed(c):
                b = c // 2
                act.wait_ge(xt_full, c + 1)
                if c:
                    act.wait_ge(v_full, c)
                nc.scalar.activation(ht[:], misc[:], ACT.Identity, bias=mod_t[:, 0, b:b + 1], scale=mod_t[:, 1, b:b + 1]).then_inc(ht_ready, 1)

            def copy_v(c):
                b = c // 2
                act.wait_ge(v_full, c + 1)
                nc.scalar.copy(v_tok[:, GPB * b:GPB * b + GPB, CT * (c % 2):CT * (c % 2) + CT, :].rearrange("p g t e -> p t g e"),
                               pv[:].rearrange("p (t g e) -> p t g e", t=CT, g=GPB)).then_inc(v_read, 1)

            def split(c):
                for ten in range(2):
                    act.wait_ge(qkt_full, 2 * c + ten + 1)
                    if c >= 2:
                        act.wait_ge(parts_out[c - 2], 16 * 6)
                    nc.scalar.copy(parts[:, c % 2, ten, 0, :], ring[:, ten, :]).then_inc(part1, 1)
                for ten in range(2):
                    act.wait_ge(res1, 2 * c + ten + 1)
                    nc.scalar.copy(parts[:, c % 2, ten, 1, :], resid[:, ten, :]).then_inc(part2, 1)

            normed(0)
            copy_v(0)
            act.wait_ge(brow_clear, 1)
            for t in range(CT):
                act.dma_start(brow[32 * t:32 * t + EXPERTS, t, :], b_ffn).then_inc(late_in, 16)
            for c in range(4):
                if c < 3:
                    normed(c + 1)
                    copy_v(c + 1)
                split(c)

            def copy_max(a, par, hl):
                u = 2 * a + par
                act.wait_ge(mtp_full, 2 * u + (1 if hl else 2))
                act.wait_ge(m_in[par][hl], 16 * a)
                nc.scalar.copy(mt[par][hl][:], misc_bf[0:GH * 3 * CT, :]).then_inc(mt_ready, 1)

            def probabilities(a, par, k, pair):
                c, j = STEPS[k]
                u = 2 * a + par
                off = max(0, P * j - CHUNK * c)
                unit = 2 * k + pair
                if pair == 0:
                    act.wait_ge(pv_done, NS * u + k + 1)
                act.wait_ge(st_full, 2 * NS * u + unit + 1)
                b0 = 2 * (unit % 2)
                nc.scalar.activation(prob[k % PRING][:, 2 * pair:2 * pair + 2, off:CHUNK], st[:, b0:b0 + 2, off:CHUNK],
                                     ACT.Exp, scale=SCALE).then_inc(p_ready, 1)

            def copy_sums(u, c, first):
                act.wait_ge(pv_done, PRING + NS * u + (8 if c else 12))
                if not first:
                    act.wait_ge(ut_full, 2 * u - (1 if c else 0))
                nc.scalar.copy(uo[c][:], pv[:]).then_inc(u_ready, 1)

            def group(a, par, first, more):
                u = 2 * a + par
                for k in range(NS):
                    probabilities(a, par, k, 0)
                    if k == 1 and not first:
                        copy_sums(u - 1, 0, False)
                    if k == 2:
                        copy_max(a, par, 0)
                    if k == 9:
                        copy_sums(u, 1, first)
                    if k == 10 and more:
                        copy_max(a + par, 1 - par, 1)
                    probabilities(a, par, k, 1)

            act.sem_inc(p_ready, 2)
            copy_max(0, 0, 1)
            group(0, 0, True, True)
            with act.Fori(0, 3) as it:
                group(it, 1, False, True)
                group(it + 1, 0, False, True)
            group(3, 1, False, False)
            copy_sums(7, 0, False)

            for e in range(4):
                b = e // 2
                act.wait_ge(at_full, e + 1)
                if e:
                    act.wait_ge(wo_full, e)
                nc.scalar.copy(att_t[:], st[:, 0, :]).then_inc(at_ready, 1)
                act.wait_ge(xt2_full, e + 1)
                if e:
                    act.wait_ge(y_full, 8 * e)
                nc.scalar.activation(h2t[:], st[:, 2, :], ACT.Identity, bias=mod_t[:, 2, b:b + 1], scale=mod_t[:, 3, b:b + 1]).then_inc(h2t_ready, 1)
                act.wait_ge(oht_full, e + 1)
                if e:
                    act.wait_ge(bias_full, e)
                nc.scalar.copy(onehot_t[:], misc[:, 0:P]).then_inc(oht_ready, 1)

        @block.vector
        def _(dve):
            dve.wait_ge(small_full, 1)
            nc.vector.tensor_copy(cond_t[:], ring[:, 0, 0:BATCH]).then_inc(dve_c, 1)
            nc.vector.tensor_scalar(sig_neg[:], st[:, 0, 0:EXPERTS], 0.0, None, ALU.is_lt).then_inc(dve_c, 1)
            dve.wait_ge(dve_c, 2)
            nc.vector.scalar_tensor_tensor(out=sign_t[:], in0=st[:, 0, 0:EXPERTS], scalar=0.0, in1=sig_neg[:],
                                           op0=ALU.is_gt, op1=ALU.subtract).then_inc(dve_c, 1)
            dve.wait_ge(exp_c, 1)
            nc.vector.tensor_scalar(cond_1[:], cond_e[:], 1.0, None, ALU.add).then_inc(dve_c, 1)
            dve.wait_ge(dve_c, 4)
            nc.vector.reciprocal(cond_r[:], cond_1[:]).then_inc(dve_c, 1)
            dve.wait_ge(dve_c, 5)
            nc.vector.tensor_tensor(silu_t[:], cond_t[:], cond_r[:], ALU.mult).then_inc(dve_c, 1)
            dve.wait_ge(dve_c, 6)
            for b in range(BATCH):
                nc.vector.tensor_scalar(silu_bc[:, b, :], ones[:], silu_t[:, b:b + 1], None, ALU.mult).then_inc(dve_c, 1)

            def norm(n, src, stat_s, aggr_s, var_s, rstd_s, out_s):
                for t in range(CT):
                    nc.vector.bn_stats(stats[:, t, :], src[:, t, :]).then_inc(stat_s, 1)
                dve.wait_ge(stat_s, CT * (n + 1))
                for t in range(CT):
                    nc.vector.bn_aggr(mv[:, t, :], stats[:, t, :]).then_inc(aggr_s, 1)
                dve.wait_ge(aggr_s, CT * (n + 1))
                nc.vector.tensor_scalar(var_eps[:], mv[:, :, 1], EPS, None, ALU.add).then_inc(var_s, 1)
                dve.wait_ge(rstd_s, n + 1)
                for t in range(CT):
                    last = nc.vector.tensor_scalar(xh[:, t, :], src[:, t, :], mv[:, t, 0:1], rstd[:, t:t + 1], ALU.subtract, ALU.mult)
                last.then_inc(out_s, 1)

            def front_norm(c):
                dve.wait_ge(x_in[c], 16)
                if c:
                    dve.wait_ge(xt_full, c)
                norm(c, x_sb[:, CT * c:CT * c + CT, :], stats_done, aggr_done, var_ready, rstd_ready, xh_ready)

            def rotate(c):
                tile0 = CT * (c % 2)
                for h in range(2):
                    dve.wait_ge(qk_full, 2 * c + h + 1)
                    if c:
                        dve.wait_ge(roped_ready, 2 * (c - 1) + h + 1)
                    bank = st[:, 2 * (c % 2) + h, :]
                    tabs = [rope_sb[:, w, tile0 + 2 * h:tile0 + 2 * h + 2, :] for w in range(2)]
                    q4 = bank.rearrange("p (t h d) -> p t h d", t=2, d=DK)
                    ob = rot_b[:, h, :, :].rearrange("p t (h d) -> p t h d", d=DK)
                    nc.vector.tensor_tensor(rot_a[:, h, :, :].rearrange("p t (h d) -> p t h d", d=DK), q4,
                                            tabs[0].rearrange("p t (o d) -> p t o d", o=1).broadcast_to([P, 2, 2 * HEADS, DK]), ALU.mult)
                    for odd in range(2):
                        last = nc.vector.tensor_tensor(
                            ob[:, :, :, odd:DK:2], q4[:, :, :, 1 - odd:DK:2],
                            tabs[1][:, :, odd:DK:2].rearrange("p t (o d) -> p t o d", o=1).broadcast_to([P, 2, 2 * HEADS, DK // 2]), ALU.mult)
                    last.then_inc(rot_ready, 1)

            def split(c):
                for ten in range(2):
                    dve.wait_ge(part1, 2 * c + ten + 1)
                    if c:
                        dve.wait_ge(part3, 2 * (c - 1) + ten + 1)
                    nc.vector.tensor_tensor(resid[:, ten, :], ring[:, ten, :], parts[:, c % 2, ten, 0, :], ALU.subtract).then_inc(res1, 1)
                for ten in range(2):
                    dve.wait_ge(part2, 2 * c + ten + 1)
                    nc.vector.tensor_tensor(parts[:, c % 2, ten, 2, :], resid[:, ten, :], parts[:, c % 2, ten, 1, :], ALU.subtract).then_inc(part3, 1)

            front_norm(0)
            dve.wait_ge(mod_full, 1)
            for n in range(4):
                last = nc.vector.tensor_scalar(mod_t[:, n, :], ring[:, 0, 16 + 2 * n:18 + 2 * n], float(n % 2), None, ALU.add)
            last.then_inc(mod_ready, 1)
            dve.wait_ge(gate_full, 1)
            nc.vector.tensor_copy(gate_raw[:].rearrange("p g d -> p (g d)"), ring[:, 1, :]).then_inc(gate_raw_ready, 1)
            front_norm(1)
            dve.wait_ge(rope_in, 16)
            rotate(0)
            for c in range(4):
                if c < 2:
                    front_norm(c + 2)
                if c < 3:
                    rotate(c + 1)
                split(c)

            def max_item(a, par, n):
                kind, half, what = ITEMS[n]
                v = 2 * a + par
                dve.wait_ge(s_full, NI * v + n + 1)
                bank = ring[:, n % 2, :]
                hl = 1 if n < NHI else 0
                t0 = CT * hl

                def to(i, pair, part):
                    return pmax[:, hl, 2 * pair + half, i - t0, part:part + 1]

                if kind == "diag":
                    i = what[0] - t0
                    last = nc.vector.tensor_reduce(pmax[:, hl, half:GH:2, i:i + 2, 0].rearrange("p s i -> p i s"),
                                                   bank.rearrange("p (i a k) -> p i a k", i=2, a=2), AX_X, ALU.max)
                elif kind == "wide":
                    i = what[0] - t0
                    last = nc.vector.tensor_reduce(pmax[:, hl, half:GH:2, i, 1], bank.rearrange("p (a k) -> p a k", a=2), AX_X, ALU.max)
                elif kind == "two":
                    i0, i1 = what[0] - t0, what[2] - t0
                    last = nc.vector.tensor_reduce(pmax[:, hl, half:GH:2, i0:i1 + 1:i1 - i0, 2].rearrange("p s i -> p i s"),
                                                   bank.rearrange("p (i a k) -> p i a k", i=2, a=2), AX_X, ALU.max)
                else:
                    last = nc.vector.tensor_reduce(to(what[0], what[1], 3), bank, AX_X, ALU.max)
                last.then_inc(s_free, 1)

            def row_max(a, par, hl):
                v = 2 * a + par
                dve.wait_ge(s_free, 2 + NI * v + (NHI if hl else NI))
                dve.wait_ge(mparts_ready, 2 * v + (1 if hl else 2) - (1 if hl else 2) ) if isinstance(a, int) and v == 0 else \
                    dve.wait_ge(mparts_ready, 2 * (v - 1) + (1 if hl else 2))
                nc.vector.tensor_reduce(rmax[hl][:], pmax[:, hl, :, :, :], AX_X, ALU.max).then_inc(rmax_ready, 1)

            def normalise(u, c):
                dve.wait_ge(ut_full, 2 * u + (2 - c))
                sums = misc[:].rearrange("p (t s e) -> p t s e", t=CT, s=GH)
                nc.vector.reciprocal(rden[c][:], sums[:, :, :, DK]).then_inc(rden_done, 1)
                dve.wait_ge(rden_done, 2 * u + (2 - c))
                out_ap = att[:, CT * c:CT * c + CT, bass.ds(u, 1), :].rearrange("p t o e -> p t (o e)")
                nc.vector.tensor_tensor(out_ap.rearrange("p t (s d) -> p t s d", s=GH), sums[:, :, :, 0:DK],
                                        rden[c][:].rearrange("p t (s o) -> p t s o", o=1).broadcast_to([P, CT, GH, DK]), ALU.mult).then_inc(att_ready, 1)

            def group(a, par, first, more):
                u = 2 * a + par
                na, npar = a + par, 1 - par
                for n in range(NI):
                    if more:
                        max_item(na, npar, n)
                    if n == NORM_AT and not first:
                        normalise(u - 1, 0)
                    if n == NHI - 1 and more:
                        row_max(na, npar, 1)
                if more:
                    row_max(na, npar, 0)
                normalise(u, 1)

            dve.sem_inc(s_free, 2)
            dve.wait_ge(const_done, 2)
            for n in range(NI):
                max_item(0, 0, n)
                if n == NHI - 1:
                    row_max(0, 0, 1)
            row_max(0, 0, 0)
            group(0, 0, True, True)
            with dve.Fori(0, 3) as it:
                group(it, 1, False, True)
                group(it + 1, 0, False, True)
            group(3, 1, False, False)
            normalise(7, 0)

            dve.sem_inc(y_used, 2)
            for e in range(4):
                dve.wait_ge(wo_full, e + 1)
                if e:
                    dve.wait_ge(acc_step, 32 * e)
                    dve.wait_ge(xt2_full, e)
                nc.vector.tensor_tensor(x2[:].rearrange("p t d -> p (t d)"), x_sb[:, CT * e:CT * e + CT, :].rearrange("p t d -> p (t d)"),
                                        st[:, 1, :], ALU.add).then_inc(x2_ready, 1)
                dve.wait_ge(x2_ready, e + 1)
                norm(e, x2, stats2, aggr2, var2, rstd2, xh2_ready)
                dve.wait_ge(sc_full, e + 1)
                sv = st[:, 3, 0:CT * EXPERTS].rearrange("p (t e) -> p t e", t=CT)
                nc.vector.tensor_reduce(smax[:], sv, AX_X, ALU.max).then_inc(route, 1)
                dve.wait_ge(route, 4 * e + 1)
                nc.vector.tensor_tensor(sc[:], sv, smax[:].rearrange("p (t o) -> p t o", o=1).broadcast_to([P, CT, EXPERTS]), ALU.is_ge).then_inc(route, 1)
                dve.wait_ge(route, 4 * e + 2)
                nc.vector.tensor_tensor(sw[:], sc[:], prio[:].rearrange("p (o e) -> p o e", o=1).broadcast_to([P, CT, EXPERTS]), ALU.mult).then_inc(route, 1)
                dve.wait_ge(route, 4 * e + 3)
                nc.vector.tensor_reduce(swm[:], sw[:], AX_X, ALU.max).then_inc(route, 1)
                dve.wait_ge(route, 4 * e + 4)
                if e:
                    dve.wait_ge(oht_full, e)
                nc.vector.tensor_tensor(onehot[:, :, 0:EXPERTS], sw[:], swm[:].rearrange("p (t o) -> p t o", o=1).broadcast_to([P, CT, EXPERTS]),
                                        ALU.is_equal).then_inc(oh_ready, 1)
                dve.wait_ge(oh_ready, e + 1)
                for t in range(CT):
                    for hf in range(2):
                        n = 8 * e + 2 * t + hf
                        dve.wait_ge(y_full, n + 1)
                        for q in range(4):
                            k = 4 * hf + q
                            step = 32 * e + 8 * t + k
                            if k:
                                dve.wait_ge(acc_step, step)
                            nc.vector.scalar_tensor_tensor(out=acc[:, t, :], in0=ring[:, n % 2, P * q:P * q + P], scalar=onehot[:, t, k:k + 1],
                                                           in1=(acc if k else x2)[:, t, :], op0=ALU.mult, op1=ALU.add).then_inc(acc_step, 1)
                        dve.wait_ge(acc_step, step + 1)
                        dve.sem_inc(y_used, 1)
                dve.wait_ge(bias_full, e + 1)
                if e >= 2:
                    dve.wait_ge(out_done[e % 2], 16)
                nc.vector.tensor_tensor(fin[e % 2][:].rearrange("p t d -> p (t d)"), acc[:].rearrange("p t d -> p (t d)"), pv[:], ALU.add).then_inc(fin_ready, 1)

        @block.gpsimd
        def _(pool):
            c_step = [0]
            own = sem("pool_own")

            def link(ins):
                c_step[0] += 1
                ins.then_inc(own, 1)
                pool.wait_ge(own, c_step[0])

            link(nc.gpsimd.memset(ones[:], 1.0))
            link(nc.gpsimd.affine_select(out=ident[:], in_=ones[:], compare_op=ALU.is_equal, fill=0.0, base=0,
                                         pattern=[[1, P]], channel_multiplier=-1))
            link(nc.gpsimd.memset(mhalf[:], -0.5))
            pool.sem_inc(const_done, 1)
            nc.gpsimd.memset(brow[:], 0.0).then_inc(brow_clear, 1)

            def as_pairs(stack):
                return stack[:].rearrange("p c s t -> p (c s t)").bitcast(F32)

            minus_ones = float(np.frombuffer(np.array([0xBF80BF80], np.uint32).tobytes(), np.float32)[0])

            def clear(i):
                nc.gpsimd.memset(as_pairs(qs[i]), 0.0).then_inc(own, 1)
                link(nc.gpsimd.memset(as_pairs(ks[i]), 0.0))
                c_step[0] += 1
                pool.wait_ge(own, c_step[0])
                link(nc.gpsimd.memset(as_pairs(ks[i])[MROW:P, :], minus_ones))

            def power(var_s, rstd_s, n):
                pool.wait_ge(var_s, n + 1)
                nc.gpsimd.tensor_tensor(rstd[:], var_eps[:], mhalf[:], ALU.pow).then_inc(rstd_s, 1)

            def add_rotated(c):
                if c:
                    pool.wait_ge(qkt_full, 2 * c)
                for h in range(2):
                    pool.wait_ge(rot_ready, 2 * c + h + 1)
                    nc.gpsimd.tensor_tensor(roped[:, 2 * h:2 * h + 2, :], rot_a[:, h, :, :], rot_b[:, h, :, :], ALU.add).then_inc(roped_ready, 1)

            nc.gpsimd.tensor_copy(ident_bf[:], ident[:]).then_inc(own, 1)
            nc.gpsimd.memset(causal[:], 0.0).then_inc(own, 1)
            for k in range(EXPERTS):
                nc.gpsimd.memset(prio[:, k:k + 1], float(EXPERTS - k)).then_inc(own, 1)
            nc.gpsimd.memset(pmax[:], -3.0e38).then_inc(own, 1)
            nc.gpsimd.memset(onehot[:], 0.0).then_inc(own, 1)
            c_step[0] += 4 + EXPERTS
            pool.wait_ge(own, c_step[0])
            link(nc.gpsimd.affine_select(out=causal[:], in_=causal[:], compare_op=ALU.is_ge, fill=NEG, base=0,
                                         pattern=[[-1, P]], channel_multiplier=1))
            power(var_ready, rstd_ready, 0)
            power(var_ready, rstd_ready, 1)
            link(nc.gpsimd.tensor_copy(causal_bf[:], causal[:].rearrange("p (o k) -> p o k", o=1).broadcast_to([P, 4, P])))
            clear(0)
            add_rotated(0)
            power(var_ready, rstd_ready, 2)
            clear(1)
            for i in range(2):
                link(nc.gpsimd.memset(vg[i][:], 0.0))
                link(nc.gpsimd.memset(vg[i][:, :, :, DK:DK + 1], 1.0))
            pool.sem_inc(const_done, 1)
            for c in range(1, 4):
                if 1 < c < 3:
                    power(var_ready, rstd_ready, c + 1)
                add_rotated(c)

            pool.wait_ge(gate_raw_ready, 1)
            nc.gpsimd.tensor_scalar(gate_sg2[:], gate_raw[:], 0.0, 2.0, ALU.is_ge, ALU.mult).then_inc(pool_g, 1)
            pool.wait_ge(pool_g, 1)
            nc.gpsimd.tensor_scalar(gate_sgn[:], gate_sg2[:], -1.0, None, ALU.add).then_inc(pool_g, 1)
            pool.wait_ge(pool_g, 2)
            nc.gpsimd.tensor_tensor(gate_abs[:], gate_raw[:], gate_sgn[:], ALU.mult).then_inc(pool_g, 1)
            pool.wait_ge(pool_g, 3)
            nc.gpsimd.tensor_scalar(gate_big[:], gate_abs[:], 0.25, None, ALU.max).then_inc(pool_g, 1)
            pool.wait_ge(pool_g, 4)
            nc.gpsimd.tensor_tensor(gate[:], gate_big[:], gate_sgn[:], ALU.mult).then_inc(pool_g, 1)
            pool.wait_ge(pool_g, 5)
            pool.wait_ge(late_in, 16 * (2 + CT))
            pool.wait_ge(const_done, 2)

            def copy_v(u, par):
                held_by(pool, v_read, 4, *([] if isinstance(u, int) and u < 2 else [(pv_done, PRING + NS * (u - 1))]))
                src = v_tok[:, u, :, :] if isinstance(u, int) else v_tok[:, bass.ds(u, 1), :, :].rearrange("p o t e -> p (o t) e")
                nc.gpsimd.tensor_copy(vg[par][:, :, :, 0:DK], src.rearrange("p t (s d) -> p t s d", s=GH)).then_inc(vg_ready, 1)

            copy_v(0, 0)

            def split_max(a, par, hl):
                u = 2 * a + par
                n = 2 * u + (0 if hl else 1)
                held_by(pool, const_done, 2, (rmax_ready, n + 1), *([] if isinstance(n, int) and n < 2 else [(mtp_full, n - 1)]))
                nc.gpsimd.tensor_copy(msp[hl][:, 0, :, :], rmax[hl][:]).then_inc(msplit, 1)
                pool.wait_ge(msplit, 3 * n + 1)
                nc.gpsimd.tensor_tensor(mres[hl][:], rmax[hl][:], msp[hl][:, 0, :, :], ALU.subtract).then_inc(msplit, 1)
                held_by(pool, const_done, 2, (msplit, 3 * n + 2))
                nc.gpsimd.tensor_copy(msp[hl][:, 1, :, :], mres[hl][:]).then_inc(msplit, 1)
                pool.wait_ge(msplit, 3 * n + 3)
                nc.gpsimd.tensor_tensor(msp[hl][:, 2, :, :], mres[hl][:], msp[hl][:, 1, :, :], ALU.subtract).then_inc(mparts_ready, 1)

            def mask(a, par, k):
                c, j = STEPS[k]
                off = P * j - CHUNK * c
                held_by(pool, const_done, 2, (p_ready, 2 * NS * (2 * a + par) + 2 * k + 2 + 2))
                d = prob[k % PRING][:, :, off:off + P]
                nc.gpsimd.affine_select(out=d, in_=d, compare_op=ALU.is_ge, fill=0.0, base=0,
                                        pattern=[[0, GH], [1, P]], channel_multiplier=-1).then_inc(masked, 1)

            def group(a, par, first, more):
                u = 2 * a + par
                if not first:
                    split_max(a, par, 0)
                if more:
                    copy_v(u + 1, 1 - par)
                for k in range(4, NS):
                    mask(a, par, k)
                    if k == 7 and more:
                        split_max(a + par, 1 - par, 1)

            split_max(0, 0, 1)
            split_max(0, 0, 0)
            for b in range(BATCH):
                nc.gpsimd.tensor_tensor(wo_g[:, b, :], wo_sb[:], gate[:, 2 * b, :], ALU.mult).then_inc(pool_g, 1)
                gb = gate[:, 2 * b + 1, :].rearrange("p (o d) -> p o d", o=1)
                nc.gpsimd.tensor_tensor(wffn_g[:, b, :, :], wffn[:], gb.broadcast_to([P, EXPERTS, D]), ALU.mult).then_inc(pool_g, 1)
                nc.gpsimd.tensor_tensor(bias_g[:, b, :, :], brow[:], gb.broadcast_to([P, CT, D]), ALU.mult).then_inc(pool_g, 1)
            pool.wait_ge(pool_g, 11)
            pool.sem_inc(gates_ready, 1)
            group(0, 0, True, True)
            with pool.Fori(0, 3) as it:
                group(it, 1, False, True)
                group(it + 1, 0, False, True)
            group(3, 1, False, False)
            for e in range(4):
                power(var2, rstd2, e)


_INS = ["L0_attn_x", "L0_attn_Wq", "L0_attn_Wk", "L0_attn_Wv", "L0_attn_Wo", "L0_ffn_tile_sigs", "L0_ffn_W", "L0_ffn_b",
        "L0_c", "L0_wmod"]


def kernel(**inputs):
    import concourse.bacc as bacc
    from concourse.bass_utils import run_bass_kernel_spmd

    nc = bacc.Bacc("TRN2", target_bir_lowering=False, num_devices=1)
    arrays, args = {}, []
    for name in _INS:
        a = np.ascontiguousarray(inputs[name])
        arrays[f"in_{name}"] = a
        args.append(nc.dram_tensor(f"in_{name}", a.shape, mybir.dt.from_np(a.dtype), kind="ExternalInput").ap())
    tables = rope_tables()
    arrays["in_rope"] = tables
    args.append(nc.dram_tensor("in_rope", tables.shape, F32, kind="ExternalInput").ap())
    out = nc.dram_tensor("out_x", (BATCH, SEQ, D), F32, kind="ExternalOutput").ap()
    adaln_block_kernel(nc, *args, out)
    r = run_bass_kernel_spmd(nc, [arrays], core_ids=[0])
    return r.results[0]["out_x"]
```

```python
from contextlib import ExitStack

import numpy as np

import concourse.bass as bass
from concourse import mybir

F32 = mybir.dt.float32
BF16 = mybir.dt.bfloat16
ALU = mybir.AluOpType
ACT = mybir.ActivationFunctionType
AX_X = mybir.AxisListType.X

P = 128
BATCH, SEQ, D = 2, 1024, 128
HEADS = 16
DK = D // HEADS
EXPERTS = 8
TILES = SEQ // P
CHUNK = 512
CT = CHUNK // P
GH = 4
GROUPS = BATCH * HEADS // GH
GPB = HEADS // GH
SCALE = float(DK) ** -0.5
EPS = 1e-5
COMBOS = 6
TAKEN_BY = ((slice(0, 3), slice(3, 6, 2), slice(4, 5)), (slice(2, 5), slice(0, 6, 5), slice(1, 2)))
SROWS = COMBOS * DK
ZROWS = 96
MROW = ZROWS
VW = 32
NEG = -1.0e30



def max_items():
    hi = [("diag", h, (i,)) for i in (4, 6) for h in (0, 1)]
    hi += [("wide", h, (6, 4)) for h in (0, 1)] + [("wide", h, (7, 5)) for h in (0, 1)]
    hi += [("two", h, (5, 4, 7, 4)) for h in (0, 1)]
    hi += [("full", h, (i, pr)) for i in range(4, 8) for pr in (0, 1) for h in (0, 1)]
    lo = [("diag", h, (i,)) for i in (0, 2) for h in (0, 1)]
    lo += [("wide", h, (2, 0)) for h in (0, 1)] + [("wide", h, (3, 1)) for h in (0, 1)]
    lo += [("two", h, (1, 0, 3, 0)) for h in (0, 1)]
    return hi, lo


HI, LO = max_items()
ITEMS = HI + LO
NI, NHI = len(ITEMS), len(HI)

STEPS = [(1, j) for j in range(8)] + [(0, j) for j in range(4)]
NS = len(STEPS)
PRING = 3
SHARE = [(1, 1, 1, 1), (0, 1, 1, 1), (0, 1, 2, 1), (0, 1, 2, 1), (0, 1, 2, 1), (0, 1, 1, 1), (0, 1, 1, 0), (0, 1, 1, 0),
         (0, 1, 1, 1), (0, 1, 1, 1), (0, 1, 1, 0), (0, 1, 1, 0)]
assert sum(map(sum, SHARE)) == NI and NS % PRING == 0
NORM_AT = sum(map(sum, SHARE[:4]))
LAG = 2


def held_by(engine, always, count, *waits):
    counts = [(s, n if isinstance(n, int) else engine.to_reg(n)) for s, n in waits]
    engine.wait_ge(always, count)
    for s, n in counts:
        engine.wait_ge(s, n)


def rope_tables():
    inv = (1.0 / np.float32(10000.0) ** (np.arange(0, DK, 2, dtype=np.float32) / np.float32(DK))).astype(np.float32)
    ang = np.outer(np.arange(SEQ, dtype=np.float32), inv).astype(np.float32)
    cos = np.repeat(np.cos(ang), 2, axis=-1)
    sin = np.repeat(np.sin(ang), 2, axis=-1)
    sin[:, 0::2] *= -1.0
    both = np.stack([cos, sin]).astype(np.float32).reshape(2, TILES, P, DK)
    return np.ascontiguousarray(both.transpose(2, 0, 1, 3))


def adaln_block_kernel(nc, x, wq, wk, wv, wo, sigs, w_ffn, b_ffn, cond, wmod, rope, out):
    x_t = x.rearrange("b (t p) d -> p (b t) d", p=P)
    out_t = out.rearrange("b (t p) d -> p (b t) d", p=P)
    parts_dram = nc.dram_tensor("parts_dram", (2, GROUPS * GH, DK, COMBOS, SEQ), BF16).ap()

    with ExitStack() as ctx:
        def sb(name, shape, dt=F32):
            return ctx.enter_context(nc.sbuf_tensor(name, shape, dt))

        def psum(name, shape):
            return ctx.enter_context(nc.psum_tensor(name, shape, F32))

        def sem(name):
            return ctx.enter_context(nc.semaphore(name))

        st = psum("st", [P, 4, CHUNK])
        ring = psum("ring", [P, 2, CHUNK])
        pv = psum("pv", [P, CHUNK])
        misc = psum("misc", [P, CHUNK])
        misc_bf = misc[:, 0:64].bitcast(BF16)

        ident = sb("ident", [P, P])
        ident_bf = sb("ident_bf", [P, P], BF16)
        causal = sb("causal", [P, P])
        causal_bf = sb("causal_bf", [P, 4, P], BF16)
        ones = sb("ones", [P, P])
        mhalf = sb("mhalf", [P, CT])
        prio = sb("prio", [P, EXPERTS])
        rope_sb = sb("rope_sb", [P, 2, TILES, DK])
        x_sb = sb("x_sb", [P, BATCH * TILES, D])
        wqkv = sb("wqkv", [P, 3 * D])
        wo_sb = sb("wo_sb", [P, D])
        wmod_sb = sb("wmod_sb", [P, 6 * D])
        wffn = sb("wffn", [P, EXPERTS, D])
        brow = sb("brow", [P, CT, D])
        small = sb("small", [P, D])
        cond_t = sb("cond_t", [P, BATCH])
        cond_e = sb("cond_e", [P, BATCH])
        cond_1 = sb("cond_1", [P, BATCH])
        cond_r = sb("cond_r", [P, BATCH])
        silu_t = sb("silu_t", [P, BATCH])
        silu_bc = sb("silu_bc", [P, BATCH, P])
        sig_neg = sb("sig_neg", [P, EXPERTS])
        sign_t = sb("sign_t", [P, EXPERTS])
        mod_t = sb("mod_t", [P, 4, BATCH])
        gate_raw = sb("gate_raw", [P, 2 * BATCH, D])
        gate_abs = sb("gate_abs", [P, 2 * BATCH, D])
        gate_big = sb("gate_big", [P, 2 * BATCH, D])
        gate_sg2 = sb("gate_sg2", [P, 2 * BATCH, D])
        gate_sgn = sb("gate_sgn", [P, 2 * BATCH, D])
        gate = sb("gate", [P, 2 * BATCH, D])
        wo_g = sb("wo_g", [P, BATCH, D])
        wffn_g = sb("wffn_g", [P, BATCH, EXPERTS, D])
        bias_g = sb("bias_g", [P, BATCH, CT, D])

        stats = sb("stats", [P, CT, 6])
        mv = sb("mv", [P, CT, 2])
        var_eps = sb("var_eps", [P, CT])
        rstd = sb("rstd", [P, CT])
        xh = sb("xh", [P, CT, D])
        ht = sb("ht", [P, CHUNK])
        rot_a = sb("rot_a", [P, 2, 2, 2 * D])
        rot_b = sb("rot_b", [P, 2, 2, 2 * D])
        roped = sb("roped", [P, CT, 2 * D])
        resid = sb("resid", [P, 2, CHUNK])
        parts = sb("parts", [P, 2, 2, 3, CHUNK], BF16)
        v_tok = sb("v_tok", [P, GROUPS, TILES, GH * DK])

        qs = [sb(f"qs{i}", [P, 2, GH, CHUNK], BF16) for i in range(2)]
        ks = [sb(f"ks{i}", [P, 2, GH, CHUNK], BF16) for i in range(2)]
        vg = [sb(f"vg{i}", [P, TILES, GH, VW]) for i in range(2)]
        prob = [sb(f"prob{i}", [P, GH, CHUNK]) for i in range(PRING)]
        pmax = sb("pmax", [P, 2, GH, CT, 4])
        rmax = [sb(f"rmax{i}", [P, GH, CT]) for i in range(2)]
        mres = [sb(f"mres{i}", [P, GH, CT]) for i in range(2)]
        msp = [sb(f"msp{i}", [P, 3, GH, CT], BF16) for i in range(2)]
        mt = [[sb(f"mt{p}{h}", [GH * 3 * CT, P], BF16) for h in range(2)] for p in range(2)]
        uo = [sb(f"uo{i}", [P, CHUNK]) for i in range(2)]
        rden = [sb(f"rden{i}", [P, CT, GH]) for i in range(2)]
        att = sb("att", [P, TILES, GROUPS, GH * DK])

        att_t = sb("att_t", [P, CHUNK])
        x2 = [sb(f"x2_{e}", [P, CT, D]) for e in range(4)]
        h2t = [sb(f"h2t{e}", [P, CHUNK]) for e in range(4)]
        sc = sb("sc", [P, CT, EXPERTS])
        smax = sb("smax", [P, CT])
        sw = sb("sw", [P, CT, EXPERTS])
        swm = sb("swm", [P, CT])
        onehot = [sb(f"onehot{e}", [P, CT, 32]) for e in range(4)]
        onehot_t = sb("onehot_t", [P, P])

        x_in = [sem(f"x_in{c}") for c in range(4)]
        small_in, wmod_in, wqkv_in, rope_in = sem("small_in"), sem("wmod_in"), sem("wqkv_in"), sem("rope_in")
        late_in = sem("late_in")
        const_done = sem("const_done")
        brow_clear = sem("brow_clear")
        small_full = sem("small_full")
        exp_c = sem("exp_c")
        dve_c = sem("dve_c")
        mod_full = sem("mod_full")
        gate_full = sem("gate_full")
        mod_ready = sem("mod_ready")
        gate_raw_ready = sem("gate_raw_ready")
        pool_g = sem("pool_g")
        stats_done, aggr_done, var_ready, rstd_ready = sem("stats_done"), sem("aggr_done"), sem("var_ready"), sem("rstd_ready")
        xh_ready, xt_full, ht_ready = sem("xh_ready"), sem("xt_full"), sem("ht_ready")
        qk_full, v_full, v_read, rot_ready, roped_ready = sem("qk_full"), sem("v_full"), sem("v_read"), sem("rot_ready"), sem("roped_ready")
        qkt_full, part1, res1, part2, part3 = sem("qkt_full"), sem("part1"), sem("res1"), sem("part2"), sem("part3")
        parts_out = [sem(f"parts_out{c}") for c in range(4)]
        kq_in = [[sem(f"kq_in{p}{h}") for h in range(2)] for p in range(2)]
        m_in = [[sem(f"m_in{p}{h}") for h in range(2)] for p in range(2)]
        s_full, s_free = sem("s_full"), sem("s_free")
        rmax_ready, msplit, mparts_ready = sem("rmax_ready"), sem("msplit"), sem("mparts_ready")
        mtp_full, mt_ready = sem("mtp_full"), sem("mt_ready")
        st_full, p_ready, masked, pv_done, vg_ready = sem("st_full"), sem("p_ready"), sem("masked"), sem("pv_done"), sem("vg_ready")
        u_ready, ut_full, rden_done, att_ready = sem("u_ready"), sem("ut_full"), sem("rden_done"), sem("att_ready")
        at_full, at_ready, wo_full, x2_ready = sem("at_full"), sem("at_ready"), sem("wo_full"), sem("x2_ready")
        stats2, aggr2, var2, rstd2, xh2_ready = sem("stats2"), sem("aggr2"), sem("var2"), sem("rstd2"), sem("xh2_ready")
        xt2_full, h2t_ready, sc_full, route, oh_ready = sem("xt2_full"), sem("h2t_ready"), sem("sc_full"), sem("route"), sem("oh_ready")
        oht_full, oht_ready, bias_full = sem("oht_full"), sem("oht_ready"), sem("bias_full")
        x2b_ready, y_full, acc_step, scaled_done = sem("x2b_ready"), sem("y_full"), sem("acc_step"), sem("scaled_done")
        pool_sum, fin_pool, out_done = sem("pool_sum"), sem("fin_pool"), sem("out_done")
        gates_ready = sem("gates_ready")

        y_banks = [st[:, i, :] for i in range(4)] + [pv[:], misc[:]]

        def y_tile(n):
            return 2 * (n % 2) + (n // 2) % 2, n // 4

        def qk_bank(c, ten):
            return ring[:, ten, :] if c < 3 else st[:, ten, :]

        block = ctx.enter_context(nc.Block())

        @block.sync
        def _(sp):
            def load_x(c):
                sp.dma_start(x_sb[:, CT * c:CT * c + CT, :], x_t[:, CT * c:CT * c + CT, :]).then_inc(x_in[c], 16)

            load_x(0)
            sp.dma_start(small[32:32 + EXPERTS, :], sigs).then_inc(small_in, 16)
            for n, w in enumerate((wq, wk, wv)):
                sp.dma_start(wqkv[:, D * n:D * n + D], w).then_inc(wqkv_in, 16)
            load_x(1)
            sp.dma_start(rope_sb[:], rope).then_inc(rope_in, 16)
            load_x(2)
            load_x(3)
            sp.dma_start(wo_sb[:], wo).then_inc(late_in, 16)
            sp.dma_start(wffn[:], w_ffn.rearrange("t d e -> d t e")).then_inc(late_in, 16)
            sp.wait_ge(brow_clear, 1)
            for t in range(CT):
                sp.dma_start(brow[32 * t:32 * t + EXPERTS, t, :], b_ffn).then_inc(late_in, 16)

            def store_parts(c):
                b = c // 2
                for part in range(3):
                    for ten in range(2):
                        sp.wait_ge((part1, part2, part3)[part], 2 * c + ten + 1)
                        dst = parts_dram[ten, HEADS * b:HEADS * b + HEADS, :, TAKEN_BY[ten][part], CHUNK * (c % 2):CHUNK * (c % 2) + CHUNK]
                        src = parts[:, c % 2, ten, part, :].rearrange("p (o t) -> p o t", o=1)
                        sp.dma_start(dst.rearrange("h d c t -> (h d) c t"),
                                     src.broadcast_to([P, (3, 2, 1)[part], CHUNK])).then_inc(parts_out[c], 16)

            def load_stacks(a, par, hl):
                lo = CHUNK * hl
                for ten, stack in ((0, qs[par]), (1, ks[par])):
                    src = parts_dram[ten, bass.ds(GH * (2 * a + par), GH), :, :, lo:lo + CHUNK]
                    sp.dma_start(stack[0:SROWS, hl, :, :], src.rearrange("h d c t -> (d c) h t")).then_inc(kq_in[par][hl], 16)

            def load_maxima(a, par, hl):
                sp.wait_ge(mt_ready, 2 * (2 * a + par) + (1 if hl else 2))
                sp.dma_start(qs[par][MROW:MROW + 3, hl, :, :], mt[par][hl][:]).then_inc(m_in[par][hl], 16)

            for c in range(2):
                store_parts(c)
            for c in range(2):
                sp.wait_ge(parts_out[1 - c], 16 * 6)
            sp.wait_ge(const_done, 2)
            for par in range(2):
                load_stacks(0, par, 1)
                load_stacks(0, par, 0)
            for c in range(2, 4):
                store_parts(c)
            load_maxima(0, 0, 1)
            for c in range(2, 4):
                sp.wait_ge(parts_out[c], 16 * 6)

            def group(a, par, loads, more):
                u = 2 * a + par
                load_maxima(a, par, 0)
                if loads:
                    held_by(sp, x_in[0], 16, (st_full, 2 * NS * u + 16))
                    load_stacks(a + 1, par, 1)
                if more:
                    load_maxima(a + par, 1 - par, 1)
                if loads:
                    held_by(sp, x_in[0], 16, (st_full, 2 * NS * (u + 1)))
                    load_stacks(a + 1, par, 0)

            group(0, 0, True, True)
            with sp.Fori(0, 2) as it:
                group(it, 1, True, True)
                group(it + 1, 0, True, True)
            group(2, 1, True, True)
            group(3, 0, False, True)
            group(3, 1, False, False)
            for e in range(4):
                sp.wait_ge(acc_step, 16 * (e + 1) if e < 3 else 80)
                if e < 3:
                    sp.wait_ge(fin_pool, e + 1)
                sp.dma_start(out_t[:, CT * e:CT * e + CT, :], x2[e][:]).then_inc(out_done, 16)
            sp.wait_ge(out_done, 64)

        @block.tensor
        def _(pe):
            pe.wait_ge(const_done, 1)
            pe.wait_ge(small_in, 32)
            pe.transpose(ring[:, 0, 0:BATCH], small[0:BATCH, :], ident[0:BATCH, 0:BATCH])
            pe.transpose(st[:, 0, 0:EXPERTS], small[32:32 + EXPERTS, :], ident[32:32 + EXPERTS, 32:32 + EXPERTS]).then_inc(small_full, 1)

            def modulation():
                pe.wait_ge(dve_c, 8)
                pe.wait_ge(wmod_in, 16)
                for n, j in enumerate((0, 1, 3, 4)):
                    last = pe.matmul(ring[:, 0, 16 + 2 * n:18 + 2 * n], wmod_sb[:, D * j:D * j + D], silu_t[:], start=True, stop=True)
                last.then_inc(mod_full, 1)
                for b in range(BATCH):
                    for n, j in enumerate((2, 5)):
                        last = pe.matmul(ring[:, 1, D * (2 * b + n):D * (2 * b + n + 1)], silu_bc[:, b, :],
                                         wmod_sb[:, D * j:D * j + D], start=True, stop=True)
                last.then_inc(gate_full, 1)

            def x_transposes(c):
                pe.wait_ge(xh_ready, c + 1)
                pe.wait_ge(ht_ready, c)
                for t in range(CT):
                    last = pe.transpose(misc[:, P * t:P * t + P], xh[:, t, :], ident[:])
                last.then_inc(xt_full, 1)

            def projections(c):
                pe.wait_ge(ht_ready, c + 1)
                if c == 0:
                    pe.wait_ge(wqkv_in, 48)
                for t in range(CT):
                    if c >= 2:
                        pe.wait_ge(rot_ready, 2 * (c - 2) + t // 2 + 1)
                    last = pe.matmul(st[:, 2 * (c % 2) + t // 2, 2 * D * (t % 2):2 * D * (t % 2 + 1)], ht[:, P * t:P * t + P],
                                     wqkv[:, 0:2 * D], start=True, stop=True)
                    if t % 2:
                        last.then_inc(qk_full, 1)
                pe.wait_ge(v_read, c)
                for t in range(CT):
                    last = pe.matmul(pv[:, P * t:P * t + P], ht[:, P * t:P * t + P], wqkv[:, 2 * D:3 * D], start=True, stop=True)
                last.then_inc(v_full, 1)

            def qk_transposes(c):
                pe.wait_ge(roped_ready, 2 * (c + 1))
                if c == 0:
                    pe.wait_ge(gate_raw_ready, 1)
                for ten in range(2):
                    if c in (1, 2):
                        pe.wait_ge(res1, 2 * (c - 1) + ten + 1)
                    if c == 3:
                        pe.wait_ge(rot_ready, 6)
                    for t in range(CT):
                        last = pe.transpose(qk_bank(c, ten)[:, P * t:P * t + P], roped[:, t, D * ten:D * ten + D], ident[:])
                    last.then_inc(qkt_full, 1)

            modulation()
            x_transposes(0)
            projections(0)
            for c in range(4):
                if c < 3:
                    x_transposes(c + 1)
                    projections(c + 1)
                    qk_transposes(c)

            def max_item(a, par, n):
                kind, half, what = ITEMS[n]
                q, k = qs[par], ks[par]
                if n == 0:
                    pe.wait_ge(kq_in[par][1], 32 * (a + 1))
                if n == NHI - 16:
                    pe.wait_ge(kq_in[par][0], 32 * (a + 1))
                pe.wait_ge(s_free, NI * (2 * a + par) + n + 1)
                bank = ring[:, n % 2, :]

                def mm(col, pair, i, j, w, start=True, stop=True):
                    return pe.matmul(bank[:, col:col + P * w], q[0:ZROWS, i // CT, 2 * pair + half, P * (i % CT):P * (i % CT) + P],
                                     k[0:ZROWS, j // CT, 2 * pair + half, P * (j % CT):P * (j % CT + w)], start=start, stop=stop)

                if kind == "diag":
                    pe.matmul(bank, ident_bf[:], causal_bf[:].rearrange("p m k -> p (m k)"), start=True, stop=False)
                for pair in range(2):
                    if kind == "diag":
                        for m in range(2):
                            last = mm(P * (2 * m + pair), pair, what[0] + m, what[0] + m, 1, start=False, stop=(pair == 1 and m == 1))
                    elif kind == "wide":
                        last = mm(2 * P * pair, pair, what[0], what[1], 2)
                    elif kind == "two":
                        for m in range(2):
                            last = mm(P * (2 * m + pair), pair, what[2 * m], what[2 * m + 1], 1)
                    elif what[1] == pair:
                        last = mm(0, pair, what[0], 0, 4)
                last.then_inc(s_full, 1)

            def max_transpose(a, par, hl):
                u = 2 * a + par
                waits = [(mparts_ready, 2 * u + (1 if hl else 2))]
                if isinstance(u, int) and u < 2 and (hl or u == 0):
                    if u or not hl:
                        waits.append((mt_ready, 2 if hl else 1))
                else:
                    waits.append((att_ready, 2 * u - (2 if hl else 1)))
                held_by(pe, const_done, 1, *waits)
                pe.transpose(misc_bf[0:GH * 3 * CT, :], msp[hl][:].rearrange("p k s i -> p (k s i)"), ident_bf[:]).then_inc(mtp_full, 1)

            def score_unit(a, par, k, pair):
                c, j = STEPS[k]
                u = 2 * a + par
                unit = 2 * k + pair
                if k == 0 and pair == 0:
                    pe.wait_ge(m_in[par][1], 16 * (a + 1))
                if k == 8 and pair == 0:
                    pe.wait_ge(m_in[par][0], 16 * (a + 1))
                pe.wait_ge(p_ready, 2 * NS * u + unit + 1)
                off = max(0, P * j - CHUNK * c)
                for half in range(2):
                    slot = 2 * pair + half
                    last = pe.matmul(st[:, 2 * (unit % 2) + half, off:CHUNK], ks[par][:, j // CT, slot, P * (j % CT):P * (j % CT) + P],
                                     qs[par][:, c, slot, off:CHUNK], start=True, stop=True)
                last.then_inc(st_full, 1)

            def weighted_sum(a, par, k):
                c, j = STEPS[k]
                u = 2 * a + par
                off = max(0, P * j - CHUNK * c)
                if k == 0:
                    pe.wait_ge(vg_ready, u + 1)
                if j == 0:
                    pe.wait_ge(u_ready, 2 * u + (1 - c))
                if P * j >= CHUNK * c:
                    pe.wait_ge(masked, 8 * u + (k - 4) + 1)
                pe.wait_ge(p_ready, 2 * NS * u + 2 * k + 2 + 2)
                for s in range(GH):
                    last = pe.matmul(pv[VW * s:VW * s + VW, off:CHUNK], vg[par][:, j, s, :], prob[k % PRING][:, s, off:CHUNK],
                                     start=(j == 0), stop=(j == (7 if c else 3)))
                last.then_inc(pv_done, 1)

            def sum_transposes(u, c):
                pe.wait_ge(u_ready, 2 * u + (2 - c))
                for t in range(CT):
                    last = pe.transpose(misc[:, P * t:P * t + P], uo[c][:, P * t:P * t + P], ident[:])
                last.then_inc(ut_full, 1)

            def out_transposes(e):
                if e == 0:
                    pe.wait_ge(s_free, 2 + NI * GROUPS)
                pe.wait_ge(att_ready, 8 if e < 2 else 16)
                pe.wait_ge(h2t_ready, e)
                for t in range(CT):
                    last = pe.transpose(ring[:, 0, P * t:P * t + P], att[:, CT * (e % 2) + t, GPB * (e // 2):GPB * (e // 2) + GPB, :].rearrange("p g e -> p (g e)"), ident[:])
                last.then_inc(at_full, 1)

            def out_projection(e):
                pe.wait_ge(at_ready, e + 1)
                pe.wait_ge(gates_ready, 1)
                pe.wait_ge(oh_ready, e)
                for t in range(CT):
                    last = pe.matmul(ring[:, 1, P * t:P * t + P], att_t[:, P * t:P * t + P], wo_g[:, e // 2, :], start=True, stop=True)
                last.then_inc(wo_full, 1)

            def norm_transposes(e):
                pe.wait_ge(xh2_ready, e + 1)
                if e:
                    pe.wait_ge(oht_ready, e)
                for t in range(CT):
                    last = pe.transpose(ring[:, 0, P * t:P * t + P], xh[:, t, :], ident[:])
                last.then_inc(xt2_full, 1)

            def routing_scores(e):
                pe.wait_ge(h2t_ready, e + 1)
                pe.wait_ge(x2b_ready, e)
                for t in range(CT):
                    last = pe.matmul(ring[:, 1, EXPERTS * t:EXPERTS * (t + 1)], h2t[e][:, P * t:P * t + P], sign_t[:], start=True, stop=True)
                last.then_inc(sc_full, 1)

            def choice_transpose(e):
                pe.wait_ge(oh_ready, e + 1)
                if e < 3:
                    pe.wait_ge(at_ready, e + 2)
                pe.transpose(ring[:, 0, 0:P], onehot[e][:].rearrange("p t e -> p (t e)"), ident[:]).then_inc(oht_full, 1)

            def chosen_bias(e):
                pe.wait_ge(oht_ready, e + 1)
                if e < 3:
                    pe.wait_ge(x2_ready, e + 2)
                pe.matmul(ring[:, 1, :], onehot_t[:], bias_g[:, e // 2, :, :].rearrange("p t e -> p (t e)"), start=True, stop=True).then_inc(bias_full, 1)

            def experts(e, *which):
                for n in which:
                    t, half = y_tile(n)
                    m = 8 * e + n
                    if m >= len(y_banks):
                        before = m - len(y_banks)
                        if before >= 24:
                            pe.wait_ge(acc_step, 48 + 8 * ((before - 24) // 2 + 1))
                        elif n % 2:
                            pe.wait_ge(scaled_done, 4 * (before // 2 + 1))
                        else:
                            pe.wait_ge(acc_step, 16 * (before // 8) + 8 * ((before % 8) // 4 + 1))
                    pe.matmul(y_banks[m % len(y_banks)], h2t[e][:, P * t:P * t + P],
                              wffn_g[:, e // 2, 4 * half:4 * half + 4, :].rearrange("p t e -> p (t e)"), start=True, stop=True).then_inc(y_full, 1)

            def group(a, par, first, more):
                u = 2 * a + par
                na, npar = a + par, 1 - par
                n = 0

                def items(count):
                    nonlocal n
                    for _ in range(count if more else 0):
                        max_item(na, npar, n)
                        n += 1

                for k in range(NS):
                    items(SHARE[k][0])
                    score_unit(a, par, k, 0)
                    items(SHARE[k][1])
                    if k >= LAG:
                        weighted_sum(a, par, k - LAG)
                    elif not first:
                        weighted_sum(a + par - 1, 1 - par, NS + k - LAG)
                    items(SHARE[k][2])
                    score_unit(a, par, k, 1)
                    items(SHARE[k][3])
                    if k == 1:
                        max_transpose(a, par, 0)
                    if k == 3 and not first:
                        pe.wait_ge(mt_ready, 2 * u + 2)
                        sum_transposes(u - 1, 0)
                    if k == 9 and more:
                        max_transpose(na, npar, 1)
                    if k == 11:
                        pe.wait_ge(*((mt_ready, 2 * u + 3) if more else (att_ready, 2 * u)))
                        sum_transposes(u, 1)
                    if not more:
                        if k == 1:
                            out_transposes(0)
                        if k == 3:
                            out_projection(0)
                        if k == 6:
                            norm_transposes(0)
                        if k == 7:
                            out_transposes(1)
                        if k == 8:
                            routing_scores(0)
                        if k == 9:
                            out_projection(1)
                        if k == 10:
                            choice_transpose(0)
                        if k == 11:
                            chosen_bias(0)

            pe.sem_inc(pv_done, PRING)
            pe.wait_ge(res1, 6)
            pe.wait_ge(const_done, 2)
            for n in range(NI):
                if n == 2:
                    qk_transposes(3)
                if n == NHI + 6:
                    max_transpose(0, 0, 1)
                max_item(0, 0, n)
            pe.wait_ge(res1, 8)
            pe.wait_ge(rot_ready, 8)
            pe.wait_ge(v_read, 4)
            group(0, 0, True, True)
            with pe.Fori(0, 3) as it:
                group(it, 1, False, True)
                group(it + 1, 0, False, True)
            group(3, 1, False, False)
            for k in range(NS - LAG, NS):
                weighted_sum(3, 1, k)
            experts(0, 0, 1)
            pe.wait_ge(att_ready, 15)
            sum_transposes(7, 0)
            for e in range(1, 5):
                experts(e - 1, *((0, 1, 2) if e > 1 else (2,)))
                if e < 4:
                    norm_transposes(e)
                experts(e - 1, 3)
                if e == 1:
                    pe.wait_ge(u_ready, 16)
                    pe.wait_ge(att_ready, 16)
                if e < 3:
                    out_transposes(e + 1)
                experts(e - 1, 4)
                if e < 4:
                    routing_scores(e)
                experts(e - 1, 5)
                if e < 3:
                    out_projection(e + 1)
                if e < 4:
                    choice_transpose(e)
                experts(e - 1, 6, 7)
                if e < 4:
                    chosen_bias(e)

        @block.scalar
        def _(act):
            act.dma_start(small[0:BATCH, :], cond).then_inc(small_in, 16)
            act.dma_start(wmod_sb[:], wmod).then_inc(wmod_in, 16)
            act.wait_ge(const_done, 1)
            nc.scalar.activation(cond_r[:], mhalf[:, 0:BATCH], ACT.Exp).then_inc(exp_c, 1)
            act.wait_ge(dve_c, 1)
            nc.scalar.activation(cond_e[:], cond_t[:], ACT.Exp, scale=-1.0).then_inc(exp_c, 1)
            act.wait_ge(mod_ready, 1)

            def normed(c):
                b = c // 2
                act.wait_ge(xt_full, c + 1)
                if c:
                    act.wait_ge(v_full, c)
                nc.scalar.activation(ht[:], misc[:], ACT.Identity, bias=mod_t[:, 0, b:b + 1], scale=mod_t[:, 1, b:b + 1]).then_inc(ht_ready, 1)

            def copy_v(c):
                b = c // 2
                act.wait_ge(v_full, c + 1)
                nc.scalar.copy(v_tok[:, GPB * b:GPB * b + GPB, CT * (c % 2):CT * (c % 2) + CT, :].rearrange("p g t e -> p t g e"),
                               pv[:].rearrange("p (t g e) -> p t g e", t=CT, g=GPB)).then_inc(v_read, 1)

            def first_parts(c):
                for ten in range(2):
                    act.wait_ge(qkt_full, 2 * c + ten + 1)
                    if c >= 2:
                        act.wait_ge(parts_out[c - 2], 16 * 6)
                    nc.scalar.copy(parts[:, c % 2, ten, 0, :], qk_bank(c, ten)).then_inc(part1, 1)

            def second_parts(c):
                for ten in range(2):
                    act.wait_ge(res1, 2 * c + ten + 1)
                    nc.scalar.copy(parts[:, c % 2, ten, 1, :], resid[:, ten, :]).then_inc(part2, 1)

            for c in range(2):
                normed(c)
                copy_v(c)
            for c in range(4):
                first_parts(c)
                if c < 2:
                    normed(c + 2)
                second_parts(c)
                if c < 2:
                    copy_v(c + 2)

            def copy_max(a, par, hl):
                u = 2 * a + par
                act.wait_ge(mtp_full, 2 * u + (1 if hl else 2))
                act.wait_ge(m_in[par][hl], 16 * a)
                nc.scalar.copy(mt[par][hl][:], misc_bf[0:GH * 3 * CT, :]).then_inc(mt_ready, 1)

            def probabilities(a, par, k, pair):
                c, j = STEPS[k]
                u = 2 * a + par
                off = max(0, P * j - CHUNK * c)
                unit = 2 * k + pair
                if pair == 0:
                    act.wait_ge(pv_done, NS * u + k + 1)
                act.wait_ge(st_full, 2 * NS * u + unit + 1)
                b0 = 2 * (unit % 2)
                nc.scalar.activation(prob[k % PRING][:, 2 * pair:2 * pair + 2, off:CHUNK], st[:, b0:b0 + 2, off:CHUNK],
                                     ACT.Exp, scale=SCALE).then_inc(p_ready, 1)

            def copy_sums(u, c, first):
                act.wait_ge(pv_done, PRING + NS * u + (8 if c else 12))
                if not first:
                    act.wait_ge(ut_full, 2 * u - (1 if c else 0))
                nc.scalar.copy(uo[c][:], pv[:]).then_inc(u_ready, 1)

            def copy_heads(e):
                act.wait_ge(at_full, e + 1)
                act.wait_ge(wo_full, e)
                nc.scalar.copy(att_t[:], ring[:, 0, :]).then_inc(at_ready, 1)

            def modulated(e):
                act.wait_ge(xt2_full, e + 1)
                nc.scalar.activation(h2t[e][:], ring[:, 0, :], ACT.Identity, bias=mod_t[:, 2, e // 2:e // 2 + 1], scale=mod_t[:, 3, e // 2:e // 2 + 1]).then_inc(h2t_ready, 1)

            def copy_choice(e):
                act.wait_ge(oht_full, e + 1)
                act.wait_ge(bias_full, e)
                nc.scalar.copy(onehot_t[:], ring[:, 0, 0:P]).then_inc(oht_ready, 1)

            def scaled_outputs(e, n):
                t, half = y_tile(n)
                act.wait_ge(y_full, 8 * e + n + 1)
                act.wait_ge(oh_ready, e + 1)
                if e >= 2:
                    act.wait_ge(fin_pool, e - 1)
                for q in range(4):
                    k = 4 * half + q
                    slot = (8 * (t - 2) + k) * P
                    nc.scalar.activation(prob[e % 2][:, slot // CHUNK, slot % CHUNK:slot % CHUNK + P],
                                         y_banks[(8 * e + n) % len(y_banks)][:, P * q:P * q + P], ACT.Identity,
                                         scale=onehot[e][:, t, k:k + 1]).then_inc(scaled_done, 1)

            def group(a, par, first, more):
                u = 2 * a + par
                for k in range(NS):
                    probabilities(a, par, k, 0)
                    if not more:
                        if k == 3:
                            copy_heads(0)
                        if k == 7:
                            modulated(0)
                        if k == 8:
                            copy_heads(1)
                        if k == 11:
                            copy_choice(0)
                    if k == 1 and not first:
                        copy_sums(u - 1, 0, False)
                    if k == 2:
                        copy_max(a, par, 0)
                    if k == 9:
                        copy_sums(u, 1, first)
                    if k == 10 and more:
                        copy_max(a + par, 1 - par, 1)
                    probabilities(a, par, k, 1)

            act.sem_inc(p_ready, 2)
            copy_max(0, 0, 1)
            group(0, 0, True, True)
            with act.Fori(0, 3) as it:
                group(it, 1, False, True)
                group(it + 1, 0, False, True)
            group(3, 1, False, False)
            copy_sums(7, 0, False)

            act.wait_ge(pv_done, PRING + NS * GROUPS)
            for e in range(1, 4):
                scaled_outputs(e - 1, 1)
                modulated(e)
                if e < 3:
                    copy_heads(e + 1)
                scaled_outputs(e - 1, 3)
                scaled_outputs(e - 1, 5)
                copy_choice(e)
                scaled_outputs(e - 1, 7)

        @block.vector
        def _(dve):
            def moments(n, src, stat_s, aggr_s, var_s):
                for t in range(CT):
                    nc.vector.bn_stats(stats[:, t, :], src[:, t, :]).then_inc(stat_s, 1)
                dve.wait_ge(stat_s, CT * (n + 1))
                for t in range(CT):
                    nc.vector.bn_aggr(mv[:, t, :], stats[:, t, :]).then_inc(aggr_s, 1)
                dve.wait_ge(aggr_s, CT * (n + 1))
                nc.vector.tensor_scalar(var_eps[:], mv[:, :, 1], EPS, None, ALU.add).then_inc(var_s, 1)

            dve.wait_ge(x_in[0], 16)
            moments(0, x_sb[:, 0:CT, :], stats_done, aggr_done, var_ready)
            dve.wait_ge(small_full, 1)
            nc.vector.tensor_copy(cond_t[:], ring[:, 0, 0:BATCH]).then_inc(dve_c, 1)
            nc.vector.tensor_scalar(sig_neg[:], st[:, 0, 0:EXPERTS], 0.0, None, ALU.is_lt).then_inc(dve_c, 1)
            dve.wait_ge(dve_c, 2)
            nc.vector.scalar_tensor_tensor(out=sign_t[:], in0=st[:, 0, 0:EXPERTS], scalar=0.0, in1=sig_neg[:],
                                           op0=ALU.is_gt, op1=ALU.subtract).then_inc(dve_c, 1)
            dve.wait_ge(exp_c, 2)
            nc.vector.tensor_scalar(cond_1[:], cond_e[:], 1.0, None, ALU.add).then_inc(dve_c, 1)
            dve.wait_ge(dve_c, 4)
            nc.vector.reciprocal(cond_r[:], cond_1[:]).then_inc(dve_c, 1)
            dve.wait_ge(dve_c, 5)
            nc.vector.tensor_tensor(silu_t[:], cond_t[:], cond_r[:], ALU.mult).then_inc(dve_c, 1)
            dve.wait_ge(dve_c, 6)
            for b in range(BATCH):
                nc.vector.tensor_scalar(silu_bc[:, b, :], ones[:], silu_t[:, b:b + 1], None, ALU.mult).then_inc(dve_c, 1)

            def norm(n, src, rstd_s, out_s):
                dve.wait_ge(rstd_s, n + 1)
                for t in range(CT):
                    last = nc.vector.tensor_scalar(xh[:, t, :], src[:, t, :], mv[:, t, 0:1], rstd[:, t:t + 1], ALU.subtract, ALU.mult)
                last.then_inc(out_s, 1)

            def front_norm(c):
                if c:
                    dve.wait_ge(x_in[c], 16)
                if c:
                    dve.wait_ge(xt_full, c)
                if c:
                    moments(c, x_sb[:, CT * c:CT * c + CT, :], stats_done, aggr_done, var_ready)
                norm(c, x_sb[:, CT * c:CT * c + CT, :], rstd_ready, xh_ready)

            def rotate(c):
                tile0 = CT * (c % 2)
                for h in range(2):
                    dve.wait_ge(qk_full, 2 * c + h + 1)
                    if c:
                        dve.wait_ge(roped_ready, 2 * (c - 1) + h + 1)
                    bank = st[:, 2 * (c % 2) + h, :]
                    tabs = [rope_sb[:, w, tile0 + 2 * h:tile0 + 2 * h + 2, :] for w in range(2)]
                    q4 = bank.rearrange("p (t h d) -> p t h d", t=2, d=DK)
                    ob = rot_b[:, h, :, :].rearrange("p t (h d) -> p t h d", d=DK)
                    nc.vector.tensor_tensor(rot_a[:, h, :, :].rearrange("p t (h d) -> p t h d", d=DK), q4,
                                            tabs[0].rearrange("p t (o d) -> p t o d", o=1).broadcast_to([P, 2, 2 * HEADS, DK]), ALU.mult)
                    for odd in range(2):
                        last = nc.vector.tensor_tensor(
                            ob[:, :, :, odd:DK:2], q4[:, :, :, 1 - odd:DK:2],
                            tabs[1][:, :, odd:DK:2].rearrange("p t (o d) -> p t o d", o=1).broadcast_to([P, 2, 2 * HEADS, DK // 2]), ALU.mult)
                    last.then_inc(rot_ready, 1)

            def split(c):
                for ten in range(2):
                    dve.wait_ge(part1, 2 * c + ten + 1)
                    if c:
                        dve.wait_ge(part3, 2 * (c - 1) + ten + 1)
                    nc.vector.tensor_tensor(resid[:, ten, :], qk_bank(c, ten), parts[:, c % 2, ten, 0, :], ALU.subtract).then_inc(res1, 1)
                for ten in range(2 if c < 2 else 0):
                    dve.wait_ge(part2, 2 * c + ten + 1)
                    nc.vector.tensor_tensor(parts[:, c % 2, ten, 2, :], resid[:, ten, :], parts[:, c % 2, ten, 1, :], ALU.subtract).then_inc(part3, 1)

            front_norm(0)
            dve.wait_ge(mod_full, 1)
            for n in range(4):
                last = nc.vector.tensor_scalar(mod_t[:, n, :], ring[:, 0, 16 + 2 * n:18 + 2 * n], float(n % 2), None, ALU.add)
            last.then_inc(mod_ready, 1)
            dve.wait_ge(gate_full, 1)
            nc.vector.tensor_copy(gate_raw[:].rearrange("p g d -> p (g d)"), ring[:, 1, :]).then_inc(gate_raw_ready, 1)
            front_norm(1)
            dve.wait_ge(rope_in, 16)
            rotate(0)
            for c in range(4):
                if c < 2:
                    front_norm(c + 2)
                if c < 3:
                    rotate(c + 1)
                    split(c)

            def max_item(a, par, n):
                kind, half, what = ITEMS[n]
                v = 2 * a + par
                dve.wait_ge(s_full, NI * v + n + 1)
                bank = ring[:, n % 2, :]
                hl = 1 if n < NHI else 0
                t0 = CT * hl

                def to(i, pair, part):
                    return pmax[:, hl, 2 * pair + half, i - t0, part:part + 1]

                if kind == "diag":
                    i = what[0] - t0
                    last = nc.vector.tensor_reduce(pmax[:, hl, half:GH:2, i:i + 2, 0].rearrange("p s i -> p i s"),
                                                   bank.rearrange("p (i a k) -> p i a k", i=2, a=2), AX_X, ALU.max)
                elif kind == "wide":
                    i = what[0] - t0
                    last = nc.vector.tensor_reduce(pmax[:, hl, half:GH:2, i, 1], bank.rearrange("p (a k) -> p a k", a=2), AX_X, ALU.max)
                elif kind == "two":
                    i0, i1 = what[0] - t0, what[2] - t0
                    last = nc.vector.tensor_reduce(pmax[:, hl, half:GH:2, i0:i1 + 1:i1 - i0, 2].rearrange("p s i -> p i s"),
                                                   bank.rearrange("p (i a k) -> p i a k", i=2, a=2), AX_X, ALU.max)
                else:
                    last = nc.vector.tensor_reduce(to(what[0], what[1], 3), bank, AX_X, ALU.max)
                last.then_inc(s_free, 1)

            def row_max(a, par, hl):
                v = 2 * a + par
                dve.wait_ge(s_free, 2 + NI * v + (NHI if hl else NI))
                if not (isinstance(v, int) and v == 0):
                    dve.wait_ge(mparts_ready, 2 * (v - 1) + (1 if hl else 2))
                nc.vector.tensor_reduce(rmax[hl][:], pmax[:, hl, :, :, :], AX_X, ALU.max).then_inc(rmax_ready, 1)

            def normalise(u, c):
                dve.wait_ge(ut_full, 2 * u + (2 - c))
                sums = misc[:].rearrange("p (t s e) -> p t s e", t=CT, s=GH)
                nc.vector.reciprocal(rden[c][:], sums[:, :, :, DK]).then_inc(rden_done, 1)
                dve.wait_ge(rden_done, 2 * u + (2 - c))
                out_ap = att[:, CT * c:CT * c + CT, bass.ds(u, 1), :].rearrange("p t o e -> p t (o e)")
                nc.vector.tensor_tensor(out_ap.rearrange("p t (s d) -> p t s d", s=GH), sums[:, :, :, 0:DK],
                                        rden[c][:].rearrange("p t (s o) -> p t s o", o=1).broadcast_to([P, CT, GH, DK]), ALU.mult).then_inc(att_ready, 1)

            def add_attention(e):
                dve.wait_ge(wo_full, e + 1)
                nc.vector.tensor_tensor(x2[e][:].rearrange("p t d -> p (t d)"), x_sb[:, CT * e:CT * e + CT, :].rearrange("p t d -> p (t d)"),
                                        ring[:, 1, :], ALU.add).then_inc(x2_ready, 1)
                dve.wait_ge(x2_ready, e + 1)
                moments(e, x2[e], stats2, aggr2, var2)

            def second_norm(e):
                dve.wait_ge(xt2_full, e)
                norm(e, x2[e], rstd2, xh2_ready)

            def routing(e):
                dve.wait_ge(sc_full, e + 1)
                sv = ring[:, 1, 0:CT * EXPERTS].rearrange("p (t e) -> p t e", t=CT)
                nc.vector.tensor_reduce(smax[:], sv, AX_X, ALU.max).then_inc(route, 1)
                dve.wait_ge(route, 4 * e + 1)
                nc.vector.tensor_tensor(sc[:], sv, smax[:].rearrange("p (t o) -> p t o", o=1).broadcast_to([P, CT, EXPERTS]), ALU.is_ge).then_inc(route, 1)
                dve.wait_ge(route, 4 * e + 2)
                nc.vector.tensor_tensor(sw[:], sc[:], prio[:].rearrange("p (o e) -> p o e", o=1).broadcast_to([P, CT, EXPERTS]), ALU.mult).then_inc(route, 1)
                dve.wait_ge(route, 4 * e + 3)
                nc.vector.tensor_reduce(swm[:], sw[:], AX_X, ALU.max).then_inc(route, 1)
                dve.wait_ge(route, 4 * e + 4)
                nc.vector.tensor_tensor(onehot[e][:, :, 0:EXPERTS], sw[:], swm[:].rearrange("p (t o) -> p t o", o=1).broadcast_to([P, CT, EXPERTS]),
                                        ALU.is_equal).then_inc(oh_ready, 1)

            def add_bias(e):
                dve.wait_ge(bias_full, e + 1)
                x2_flat = x2[e][:].rearrange("p t d -> p (t d)")
                nc.vector.tensor_tensor(x2_flat, x2_flat, ring[:, 1, :], ALU.add).then_inc(x2b_ready, 1)

            def add_experts(e, half):
                if half == 0:
                    dve.wait_ge(x2b_ready, e + 1)
                    dve.wait_ge(oh_ready, e + 1)
                for q in range(4):
                    for t in range(2):
                        n, k = 4 * half + 2 * t, 4 * half + q
                        if q == 0:
                            dve.wait_ge(y_full, 8 * e + n + 1)
                        if k:
                            dve.wait_ge(acc_step, 16 * e + 2 * k + t - 1)
                        nc.vector.scalar_tensor_tensor(out=x2[e][:, t, :], in0=y_banks[(8 * e + n) % len(y_banks)][:, P * q:P * q + P],
                                                       scalar=onehot[e][:, t, k:k + 1], in1=x2[e][:, t, :], op0=ALU.mult, op1=ALU.add).then_inc(acc_step, 1)

            def group(a, par, first, more):
                u = 2 * a + par
                na, npar = a + par, 1 - par
                for n in range(NI):
                    if more:
                        max_item(na, npar, n)
                    elif n == 0:
                        add_attention(0)
                        second_norm(0)
                    if n == NORM_AT and not first:
                        normalise(u - 1, 0)
                    if n == NHI - 1 and more:
                        row_max(na, npar, 1)
                if more:
                    row_max(na, npar, 0)
                else:
                    routing(0)
                    add_attention(1)
                    second_norm(1)
                normalise(u, 1)

            dve.sem_inc(s_free, 2)
            dve.wait_ge(const_done, 2)
            for n in range(NI):
                if n == 6:
                    split(3)
                max_item(0, 0, n)
                if n == NHI - 1:
                    row_max(0, 0, 1)
            row_max(0, 0, 0)
            group(0, 0, True, True)
            with dve.Fori(0, 3) as it:
                group(it, 1, False, True)
                group(it + 1, 0, False, True)
            group(3, 1, False, False)
            normalise(7, 0)

            add_bias(0)
            for e in range(1, 4):
                add_experts(e - 1, 0)
                routing(e)
                if e < 3:
                    add_attention(e + 1)
                add_experts(e - 1, 1)
                if e < 3:
                    second_norm(e + 1)
                add_bias(e)
            dve.wait_ge(x2b_ready, 4)
            for n in range(0, 8, 2):
                for q in range(4):
                    for i in range(2):
                        t, half = y_tile(n + i)
                        if q == 0:
                            dve.wait_ge(y_full, 24 + n + i + 1)
                        step = 48 + 4 * n + 2 * q + i
                        dve.wait_ge(acc_step, step - 1 if q else 48 + 4 * n)
                        x2_tile = x2[3][:, t, :]
                        nc.vector.scalar_tensor_tensor(out=x2_tile, in0=y_banks[(24 + n + i) % len(y_banks)][:, P * q:P * q + P],
                                                       scalar=onehot[3][:, t, 4 * half + q:4 * half + q + 1], in1=x2_tile,
                                                       op0=ALU.mult, op1=ALU.add).then_inc(acc_step, 1)

        @block.gpsimd
        def _(pool):
            c_step = [0]
            own = sem("pool_own")

            def link(ins):
                c_step[0] += 1
                ins.then_inc(own, 1)
                pool.wait_ge(own, c_step[0])

            link(nc.gpsimd.memset(ones[:], 1.0))
            link(nc.gpsimd.affine_select(out=ident[:], in_=ones[:], compare_op=ALU.is_equal, fill=0.0, base=0,
                                         pattern=[[1, P]], channel_multiplier=-1))
            link(nc.gpsimd.memset(mhalf[:], -0.5))
            pool.sem_inc(const_done, 1)
            nc.gpsimd.memset(brow[:], 0.0).then_inc(brow_clear, 1)

            def as_pairs(stack):
                return stack[:].rearrange("p c s t -> p (c s t)").bitcast(F32)

            minus_ones = float(np.frombuffer(np.array([0xBF80BF80], np.uint32).tobytes(), np.float32)[0])

            def clear(i):
                nc.gpsimd.memset(as_pairs(qs[i]), 0.0).then_inc(own, 1)
                link(nc.gpsimd.memset(as_pairs(ks[i]), 0.0))
                c_step[0] += 1
                pool.wait_ge(own, c_step[0])
                link(nc.gpsimd.memset(as_pairs(ks[i])[MROW:P, :], minus_ones))

            def power(var_s, rstd_s, n):
                pool.wait_ge(var_s, n + 1)
                nc.gpsimd.tensor_tensor(rstd[:], var_eps[:], mhalf[:], ALU.pow).then_inc(rstd_s, 1)

            def add_rotated(c):
                if c:
                    pool.wait_ge(qkt_full, 2 * c)
                for h in range(2):
                    pool.wait_ge(rot_ready, 2 * c + h + 1)
                    nc.gpsimd.tensor_tensor(roped[:, 2 * h:2 * h + 2, :], rot_a[:, h, :, :], rot_b[:, h, :, :], ALU.add).then_inc(roped_ready, 1)

            def third_parts(c):
                for ten in range(2):
                    pool.wait_ge(part2, 2 * c + ten + 1)
                    nc.gpsimd.tensor_tensor(parts[:, c % 2, ten, 2, :], resid[:, ten, :], parts[:, c % 2, ten, 1, :], ALU.subtract).then_inc(part3, 1)

            nc.gpsimd.tensor_copy(ident_bf[:], ident[:]).then_inc(own, 1)
            nc.gpsimd.memset(causal[:], 0.0).then_inc(own, 1)
            for k in range(EXPERTS):
                nc.gpsimd.memset(prio[:, k:k + 1], float(EXPERTS - k)).then_inc(own, 1)
            nc.gpsimd.memset(pmax[:], -3.0e38).then_inc(own, 1)
            for e in range(4):
                nc.gpsimd.memset(onehot[e][:], 0.0).then_inc(own, 1)
            c_step[0] += 7 + EXPERTS
            pool.wait_ge(own, c_step[0])
            link(nc.gpsimd.affine_select(out=causal[:], in_=causal[:], compare_op=ALU.is_ge, fill=NEG, base=0,
                                         pattern=[[-1, P]], channel_multiplier=1))
            power(var_ready, rstd_ready, 0)
            clear(0)
            power(var_ready, rstd_ready, 1)
            add_rotated(0)
            power(var_ready, rstd_ready, 2)
            link(nc.gpsimd.tensor_copy(causal_bf[:], causal[:].rearrange("p (o k) -> p o k", o=1).broadcast_to([P, 4, P])))
            for i in range(2):
                link(nc.gpsimd.memset(vg[i][:], 0.0))
                link(nc.gpsimd.memset(vg[i][:, :, :, DK:DK + 1], 1.0))
            add_rotated(1)
            power(var_ready, rstd_ready, 3)
            clear(1)
            pool.sem_inc(const_done, 1)
            add_rotated(2)
            add_rotated(3)
            third_parts(2)
            third_parts(3)

            pool.wait_ge(gate_raw_ready, 1)
            nc.gpsimd.tensor_scalar(gate_sg2[:], gate_raw[:], 0.0, 2.0, ALU.is_ge, ALU.mult).then_inc(pool_g, 1)
            pool.wait_ge(pool_g, 1)
            nc.gpsimd.tensor_scalar(gate_sgn[:], gate_sg2[:], -1.0, None, ALU.add).then_inc(pool_g, 1)
            pool.wait_ge(pool_g, 2)
            nc.gpsimd.tensor_tensor(gate_abs[:], gate_raw[:], gate_sgn[:], ALU.mult).then_inc(pool_g, 1)
            pool.wait_ge(pool_g, 3)
            nc.gpsimd.tensor_scalar(gate_big[:], gate_abs[:], 0.25, None, ALU.max).then_inc(pool_g, 1)
            pool.wait_ge(pool_g, 4)
            nc.gpsimd.tensor_tensor(gate[:], gate_big[:], gate_sgn[:], ALU.mult).then_inc(pool_g, 1)
            pool.wait_ge(pool_g, 5)
            pool.wait_ge(late_in, 16 * (2 + CT))
            pool.wait_ge(const_done, 2)

            def copy_v(u, par):
                held_by(pool, v_read, 4, *([] if isinstance(u, int) and u < 2 else [(pv_done, PRING + NS * (u - 1))]))
                src = v_tok[:, u, :, :] if isinstance(u, int) else v_tok[:, bass.ds(u, 1), :, :].rearrange("p o t e -> p (o t) e")
                nc.gpsimd.tensor_copy(vg[par][:, :, :, 0:DK], src.rearrange("p t (s d) -> p t s d", s=GH)).then_inc(vg_ready, 1)

            copy_v(0, 0)

            def split_max(a, par, hl):
                u = 2 * a + par
                n = 2 * u + (0 if hl else 1)
                held_by(pool, const_done, 2, (rmax_ready, n + 1), *([] if isinstance(n, int) and n < 2 else [(mtp_full, n - 1)]))
                nc.gpsimd.tensor_copy(msp[hl][:, 0, :, :], rmax[hl][:]).then_inc(msplit, 1)
                pool.wait_ge(msplit, 3 * n + 1)
                nc.gpsimd.tensor_tensor(mres[hl][:], rmax[hl][:], msp[hl][:, 0, :, :], ALU.subtract).then_inc(msplit, 1)
                held_by(pool, const_done, 2, (msplit, 3 * n + 2))
                nc.gpsimd.tensor_copy(msp[hl][:, 1, :, :], mres[hl][:]).then_inc(msplit, 1)
                pool.wait_ge(msplit, 3 * n + 3)
                nc.gpsimd.tensor_tensor(msp[hl][:, 2, :, :], mres[hl][:], msp[hl][:, 1, :, :], ALU.subtract).then_inc(mparts_ready, 1)

            def mask(a, par, k):
                c, j = STEPS[k]
                off = P * j - CHUNK * c
                held_by(pool, const_done, 2, (p_ready, 2 * NS * (2 * a + par) + 2 * k + 2 + 2))
                d = prob[k % PRING][:, :, off:off + P]
                nc.gpsimd.affine_select(out=d, in_=d, compare_op=ALU.is_ge, fill=0.0, base=0,
                                        pattern=[[0, GH], [1, P]], channel_multiplier=-1).then_inc(masked, 1)

            def group(a, par, first, more):
                u = 2 * a + par
                if not first:
                    split_max(a, par, 0)
                if more:
                    copy_v(u + 1, 1 - par)
                for k in range(4, NS):
                    mask(a, par, k)
                    if k == 7 and more:
                        split_max(a + par, 1 - par, 1)
                    if not more and k in (4, 10):
                        power(var2, rstd2, (k - 4) // 6)

            split_max(0, 0, 1)
            split_max(0, 0, 0)
            for b in range(BATCH):
                nc.gpsimd.tensor_tensor(wo_g[:, b, :], wo_sb[:], gate[:, 2 * b, :], ALU.mult).then_inc(pool_g, 1)
                gb = gate[:, 2 * b + 1, :].rearrange("p (o d) -> p o d", o=1)
                nc.gpsimd.tensor_tensor(wffn_g[:, b, :, :], wffn[:], gb.broadcast_to([P, EXPERTS, D]), ALU.mult).then_inc(pool_g, 1)
                nc.gpsimd.tensor_tensor(bias_g[:, b, :, :], brow[:], gb.broadcast_to([P, CT, D]), ALU.mult).then_inc(pool_g, 1)
            pool.wait_ge(pool_g, 11)
            pool.sem_inc(gates_ready, 1)
            group(0, 0, True, True)
            with pool.Fori(0, 3) as it:
                group(it, 1, False, True)
                group(it + 1, 0, False, True)
            group(3, 1, False, False)

            def add_scaled(e):
                s = prob[e % 2][:].rearrange("p s c -> p (s c)").rearrange("p (t k d) -> p t k d", t=2, k=EXPERTS)
                pool.wait_ge(scaled_done, 16 * (e + 1))
                for i, w in enumerate((4, 2, 1)):
                    if i:
                        pool.wait_ge(pool_sum, 3 * e + i)
                    nc.gpsimd.tensor_tensor(s[:, :, 0:w, :], s[:, :, 0:w, :], s[:, :, w:2 * w, :], ALU.add).then_inc(pool_sum, 1)
                pool.wait_ge(pool_sum, 3 * e + 3)
                pool.wait_ge(x2b_ready, e + 1)
                nc.gpsimd.tensor_tensor(x2[e][:, 2:4, :], x2[e][:, 2:4, :], s[:, :, 0, :], ALU.add).then_inc(fin_pool, 1)

            for e in range(1, 4):
                if e < 3:
                    power(var2, rstd2, e + 1)
                add_scaled(e - 1)


_INS = ["L0_attn_x", "L0_attn_Wq", "L0_attn_Wk", "L0_attn_Wv", "L0_attn_Wo", "L0_ffn_tile_sigs", "L0_ffn_W", "L0_ffn_b",
        "L0_c", "L0_wmod"]


def kernel(**inputs):
    import concourse.bacc as bacc
    from concourse.bass_utils import run_bass_kernel_spmd

    nc = bacc.Bacc("TRN2", target_bir_lowering=False, num_devices=1)
    arrays, args = {}, []
    for name in _INS:
        a = np.ascontiguousarray(inputs[name])
        arrays[f"in_{name}"] = a
        args.append(nc.dram_tensor(f"in_{name}", a.shape, mybir.dt.from_np(a.dtype), kind="ExternalInput").ap())
    tables = rope_tables()
    arrays["in_rope"] = tables
    args.append(nc.dram_tensor("in_rope", tables.shape, F32, kind="ExternalInput").ap())
    out = nc.dram_tensor("out_x", (BATCH, SEQ, D), F32, kind="ExternalOutput").ap()
    adaln_block_kernel(nc, *args, out)
    r = run_bass_kernel_spmd(nc, [arrays], core_ids=[0])
    return r.results[0]["out_x"]
```
